# Optimizing a Trainium2 kernel written in Bass

```python
import numpy as np
import jax
import jax.numpy as jnp

def _softmax(x, axis=-1):
    return jax.nn.softmax(x, axis=axis)
def _gelu(x):
    return jax.nn.gelu(x, approximate=True)
def _silu(x):
    return jax.nn.silu(x)
def _sigmoid(x):
    return jax.nn.sigmoid(x)
def _layernorm(x, axis=-1, eps=1e-5):
    m = jnp.mean(x, axis=axis, keepdims=True)
    v = jnp.var(x, axis=axis, keepdims=True)
    return (x - m) / jnp.sqrt(v + eps)
def _scatter_add(tgt, idx, src, axis=0):
    return tgt.at[idx].add(src)
def _segment_sum(src, seg, n):
    return jax.ops.segment_sum(src, seg, n)

kernel_name = 'mk_conv_seq_d1_conv_nhwc64_cd6556'

def setup_inputs(seed: int = 0):
    np.random.seed(seed)
    _w = jnp.asarray
    def _rec_inputs():
        import jax
        import jax.numpy as jnp
        _gk = jax.random.key(seed)
        x = -7.109e-05 + 0.9999 * jax.random.normal(jax.random.fold_in(_gk, 1), (16, 256, 256, 64), jnp.float32)
        return x
    x = _rec_inputs()
    def _L0_conv_setup():
        import jax, jax.numpy as jnp
        import numpy as np
        B, H, W, C = (16, 256, 256, 64)
        M1, M2 = (20, 20)
        key = jax.random.key(seed)
        k1, k2, k3, k4 = jax.random.split(key, 4)
        std = 5.0 / 3.0 * np.sqrt(2.0 / (C + C))
        points = jax.random.normal(k1, (B, H, W, C), dtype=jnp.float32)
        kernel_real = std * jax.random.normal(k2, (M1, M2, C, C), dtype=jnp.float32)
        kernel_imag = std * jax.random.normal(k3, (M1, M2, C, C), dtype=jnp.float32)
        w_lin = jax.random.normal(k4, (C, C), dtype=jnp.float32) / np.sqrt(C)
        return {'points': points, 'kernel_real': kernel_real, 'kernel_imag': kernel_imag, 'w_lin': w_lin}
    _L0_conv_all = _L0_conv_setup()
    _L0_conv_in = {k: v for k, v in _L0_conv_all.items() if k in ('kernel_real', 'kernel_imag', 'w_lin', )}
    del _L0_conv_all

    return {
        "x": x,
        "L0_conv_kernel_real": _L0_conv_in["kernel_real"],
        "L0_conv_kernel_imag": _L0_conv_in["kernel_imag"],
        "L0_conv_w_lin": _L0_conv_in["w_lin"],
    }

def reference(x, L0_conv_kernel_real, L0_conv_kernel_imag, L0_conv_w_lin):
    import jax
    import jax.numpy as jnp
    def _L0_conv_ref(points, kernel_real, kernel_imag, w_lin):
        import jax, jax.numpy as jnp
        import numpy as np
        B, H, W, C = (16, 256, 256, 64)
        M1, M2 = (20, 20)
        kernel = kernel_real + 1j * kernel_imag
        fft = jnp.fft.rfftn(points, axes=(1, 2))
        idx1 = jnp.concatenate([jnp.arange(H - M1 // 2, H), jnp.arange(0, M1 // 2)])
        modes = fft[:, idx1, :M2, :]
        modes = jnp.einsum('xyij,bxyj->bxyi', kernel, modes)
        Wr = W // 2 + 1
        spec = jnp.zeros((B, H, Wr, C), dtype=fft.dtype)
        spec = spec.at[:, idx1, :M2, :].set(modes)
        ifft = jnp.fft.irfftn(spec, s=(H, W), axes=(1, 2))
        return ifft + points @ w_lin.T + points

    def _gn(v, G=32, eps=1e-5):
        B_, H_, W_, C_ = v.shape
        g = v.reshape(B_, H_, W_, G, C_ // G)
        m = jnp.mean(g, axis=(1, 2, 4), keepdims=True)
        s = jnp.var(g, axis=(1, 2, 4), keepdims=True)
        return ((g - m) / jnp.sqrt(s + eps)).reshape(v.shape)

    def _ln_c(v, eps=1e-6):
        m = jnp.mean(v, axis=-1, keepdims=True)
        s = jnp.var(v, axis=-1, keepdims=True)
        return (v - m) / jnp.sqrt(s + eps)

    def _ln_t(v, eps=1e-5):
        m = jnp.mean(v, axis=-1, keepdims=True)
        s = jnp.var(v, axis=-1, keepdims=True)
        return (v - m) / jnp.sqrt(s + eps)

    def _to_tokens(v):
        B_, H_, W_, C_ = v.shape
        return v.reshape(B_, H_ * W_, C_)
    def _from_tokens(t, like):
        return t.reshape(like.shape)

    x = _L0_conv_ref(x, L0_conv_kernel_real, L0_conv_kernel_imag, L0_conv_w_lin)
    return x


_drawn_inputs = setup_inputs


def setup_inputs(seed=0):
    import zlib

    import numpy as np

    out = dict(_drawn_inputs(seed))
    spreads = {}
    factors = {}
    for name, (base, spread) in spreads.items():
        noise = np.random.default_rng([zlib.crc32(name.encode()), seed]).standard_normal(out[name].shape)
        drawn = base * np.exp(spread * noise) if base else spread * noise
        out[name] = jnp.asarray(drawn.astype(out[name].dtype))
    for name, factor in factors.items():
        out[name] = (out[name] * factor).astype(out[name].dtype)
    return out
```

```python
from contextlib import ExitStack

import concourse.bass as bass
from concourse import mybir

F32 = mybir.dt.float32
BF16 = mybir.dt.bfloat16
ALU = mybir.AluOpType

P = 128
H = W = 256
C = 64
KX = 20
KP = 11
ROWS = 2 * KP - 1
MODES_Y = 20
TILE_W = 32
TILE = TILE_W * C
SLOTS = 8
TILES = 2 * W // TILE_W
UNIT = 512
UNITS = TILES * TILE // UNIT
GROUPS = 16
BROWS = 6 * ROWS
SROWS = 3 * 2 * KX
YCOLS = 4 * 2 * KX


def wait(eng, sem, value):
    if not (isinstance(value, int) and value <= 0):
        eng.wait_ge(sem, value)


def sub(base, offset, dims):
    return bass.AP(base.tensor, base.offset + offset, [list(base.ap[0])] + dims)


def spectral_conv(nc, x, k_re, k_im, w_lin, t_h, t_w, t_id, t_sel, t_iw, t_ih, t_part, out):
    NB = x.shape[0]
    BH = NB // 2
    RB = NB * YCOLS
    SB = 2 * C * ROWS
    with ExitStack() as ctx:
        def sb(name, shape, dt):
            return ctx.enter_context(nc.sbuf_tensor(name, shape, dt))

        def sem(name):
            return ctx.enter_context(nc.semaphore(name))

        bank = [ctx.enter_context(nc.psum_tensor(f"bank{i}", [P, UNIT], F32)) for i in range(8)]

        dft_h = sb("dft_h", [P, 2, 32], F32)
        dft_w = sb("dft_w", [P, 2, 4, 2 * KX], F32)
        ident = sb("ident", [P, P], F32)
        sel = sb("sel", [P, C], BF16)
        inv_w = sb("inv_w", [SROWS, 2, W], BF16)
        inv_h = sb("inv_h", [BROWS, 2, P], BF16)
        part = sb("part", [BROWS, 2], F32)
        zero = sb("zero", [P, C], F32)
        w_nat = sb("w_nat", [P, P], F32)
        w_blk = sb("w_blk", [P, P], F32)

        ring = sb("ring", [P, SLOTS * TILE], F32)
        KN = MODES_Y * C * C // P
        kbuf = [ring[:, q * 3 * KN:(q + 1) * 3 * KN] for q in range(2)]
        at = 6 * KN
        lbuf = [ring[:, at + q * 4 * KN:at + (q + 1) * 4 * KN] for q in range(2)]
        at += 8 * KN
        ypart = ring[:, at:at + RB].bitcast(BF16)
        at += RB
        ysum = ring[:, at:at + 2 * KX * NB]
        at += 2 * KX * NB
        yrest = ring[:, at:at + 2 * KX * NB]
        at += 2 * KX * NB
        yminus = ring[:, at:at + KX * NB]
        assert at + KX * NB <= SLOTS * TILE

        half_buf = sb("half_buf", [P, 2 * P * C], BF16)
        bst = [half_buf[0:BROWS, h * P * C:(h + 1) * P * C] for h in range(2)]
        modes = half_buf[:, 0:2 * 2 * KP * KX * NB].bitcast(F32)

        spec = sb("spec", [P, max(16, NB) * SB], BF16)
        hrow = spec[:, 0:2 * 16 * W].bitcast(F32)
        hcol = spec[:, 2 * 16 * W:2 * 16 * W + 4 * ROWS * C].bitcast(F32)

        xt = sb("xt", [P, 2, UNIT], F32)
        copies = sb("copies", [SROWS, 2, 8 * BROWS], BF16)
        b1 = sb("b1", [BROWS, 2, UNIT], BF16)
        brest = sb("brest", [BROWS, 2, UNIT], F32)
        b2 = sb("b2", [BROWS, 2, UNIT], BF16)

        tables_in = sem("tables_in")
        cast_in = sem("cast_in")
        w_zeroed = sem("w_zeroed")
        w_turned = sem("w_turned")
        w_ready = sem("w_ready")
        x_in = [sem(f"x_in{s}") for s in range(SLOTS)]
        h_done = sem("h_done")
        h_evac = sem("h_evac")
        turn_done = sem("turn_done")
        turn_act = sem("turn_act")
        turn_dve = sem("turn_dve")
        w_done = sem("w_done")
        modes_in = sem("modes_in")
        k_in = [sem(f"k_in{q}") for q in range(2)]
        k_neg = sem("k_neg")
        kt_group = sem("kt_group")
        kt_act = sem("kt_act")
        kt_dve = sem("kt_dve")
        mix_done = sem("mix_done")
        yminus_in = sem("yminus_in")
        ysum_in = sem("ysum_in")
        y1_in = sem("y1_in")
        yrest_in = sem("yrest_in")
        y2_in = sem("y2_in")
        y3_in = sem("y3_in")
        zeroed = sem("zeroed")
        s_done = sem("s_done")
        s_act = sem("s_act")
        s_dve = sem("s_dve")
        xt_done = sem("xt_done")
        xt_in = sem("xt_in")
        unit_done = sem("unit_done")
        added = sem("added")
        stored = [sem(f"stored{s}") for s in range(SLOTS)]
        copies_in = sem("copies_in")
        iw_done = sem("iw_done")
        b1_in = sem("b1_in")
        brest_in = sem("brest_in")
        b2_in = sem("b2_in")
        b_in = sem("b_in")

        def slot(s):
            return ring[:, s * TILE:(s + 1) * TILE]

        def x_tile(t, b, j):
            hh, wq = j % 2, j // 2
            return t[bass.ds(b, 1), hh * P:(hh + 1) * P, wq * TILE_W:(wq + 1) * TILE_W, :].rearrange(
                "b h w c -> h (b w c)")

        block = ctx.enter_context(nc.Block())

        @block.sync
        def _(sp):
            def load(b, j):
                sp.dma_start(slot(j % SLOTS), x_tile(x, b, j)).then_inc(x_in[j % SLOTS], 16)

            for dst, src in ((dft_h, t_h), (ident, t_id)):
                sp.dma_start(dst[:], src).then_inc(tables_in, 16)
            for j in range(SLOTS):
                load(0, j)
            for dst, src in ((dft_w, t_w), (part, t_part)):
                sp.dma_start(dst[:], src).then_inc(tables_in, 16)
            sp.wait_ge(w_zeroed, 1)
            for e in range(2):
                sp.dma_start(w_nat[e * C:(e + 1) * C, e * C:(e + 1) * C], w_lin).then_inc(tables_in, 16)

            def forward(b, last):
                for t in range(TILES // 2):
                    later = t + SLOTS // 2
                    if last and later >= TILES // 2:
                        break
                    sp.wait_ge(h_done, b * (TILES // 2) + t + 1)
                    for hh in range(2):
                        if later < TILES // 2:
                            load(b, 2 * later + hh)
                        else:
                            load(b + 1, 2 * (later - TILES // 2) + hh)

            with sp.Fori(0, NB - 1) as b:
                forward(b, False)
            forward(NB - 1, True)

            def kernels(q, row, order):
                for t, src in enumerate((k_im, k_re)):
                    flat = src[bass.ds(row, 1)].rearrange("x y i j -> (x y i) j").rearrange("(s p) j -> p s j", p=P)
                    dst = kbuf[q].rearrange("p (s t j) -> p s t j", t=3, j=C)[:, :, t, :]
                    sp.dma_start(dst, flat).then_inc(k_in[q], 16)

            sp.wait_ge(h_done, NB * (TILES // 2))
            kernels(0, 10, 0)
            kernels(1, 11, 1)
            sp.wait_ge(kt_group, 6)
            kernels(0, 9, 2)
            with sp.Fori(2, 10) as k:
                minus_k = sp.snap(k * -1 + 10)
                sp.wait_ge(kt_group, 6 * (2 * k - 2))
                kernels(1, 10 + k, 2 * k - 1)
                sp.wait_ge(kt_group, 6 * (2 * k - 1))
                kernels(0, minus_k, 2 * k)
            sp.wait_ge(kt_group, 6 * 18)
            kernels(1, 0, 19)

            sp.wait_ge(s_done, 8 * 10 + 4)
            for j in range(SLOTS):
                load(0, j)

            def inverse(b, first, last):
                for j in range(TILES):
                    sp.wait_ge(added, b * UNITS + 4 * (j + 1))
                    sp.dma_start(x_tile(out, b, j), slot(j % SLOTS)).then_inc(stored[j % SLOTS], 16)
                    if (first and j == 0) or (last and j + SLOTS - 1 >= TILES):
                        continue
                    before = (j - 1) % SLOTS
                    n = 2 * b + (j - 1) // SLOTS + 1
                    sp.wait_ge(stored[before], 16 * n)
                    j2 = j + SLOTS - 1
                    load(b if j2 < TILES else b + 1, j2 % TILES)

            inverse(0, True, False)
            with sp.Fori(1, NB - 1) as b:
                inverse(b, False, False)
            inverse(NB - 1, False, True)
            for s in range(SLOTS):
                sp.wait_ge(stored[s], 16 * 2 * NB)

        @block.gpsimd
        def _(pool):
            pool.memset(w_nat[:], 0.0).then_inc(w_zeroed, 1)
            for dst, src in ((sel, t_sel), (inv_w, t_iw), (inv_h, t_ih)):
                pool.dma_start(dst[:], src).then_inc(cast_in, 16)
            pool.wait_ge(h_done, NB * (TILES // 2))
            pool.memset(ypart, 0.0).then_inc(zeroed, 1)
            pool.memset(zero[:], 0.0).then_inc(zeroed, 1)
            pool.wait_ge(zeroed, 2)

            def negate(q, count):
                pool.wait_ge(k_in[q], 32 * count)
                of = kbuf[q].rearrange("p (s t j) -> p s t j", t=3, j=C)
                pool.tensor_tensor(of[:, :, 2, :], sub(zero[:], 0, [[0, 10], [1, C]]), of[:, :, 0, :],
                                   ALU.subtract).then_inc(k_neg, 1)

            negate(0, 1)
            negate(1, 1)
            negate(0, 2)
            with pool.Fori(2, 10) as k:
                negate(1, k)
                negate(0, k + 1)
            negate(1, 10)

        @block.tensor
        def _(pe):
            pe.wait_ge(tables_in, 6 * 16)
            pe.wait_ge(cast_in, 3 * 16)
            pe.transpose(bank[7][:, 0:P], w_nat[:], ident[:]).then_inc(w_turned, 1)

            def forward(b):
                for t in range(TILES // 2):
                    for hh in range(2):
                        s = 2 * (t % (SLOTS // 2)) + hh
                        pe.wait_ge(x_in[s], 16 * (2 * b + t // (SLOTS // 2) + 1))
                    if t > 1:
                        pe.wait_ge(h_evac, b * (TILES // 2) + t - 1)
                    for hh in range(2):
                        tile = slot(2 * (t % (SLOTS // 2)) + hh).rearrange("p (w c) -> p w c", c=C)
                        for g in range(4):
                            last = pe.matmul(bank[t % 2][32 * g:32 * g + 32, :], dft_h[:, hh, :],
                                             tile[:, :, 16 * g:16 * g + 16], start=hh == 0, stop=hh == 1,
                                             tile_position=(0, 32 * g))
                    last.then_inc(h_done, 1)
                pe.wait_ge(h_evac, (b + 1) * (TILES // 2))
                for j in range(8):
                    if j >= 4:
                        pe.wait_ge(turn_act if j % 2 else turn_dve, 4 * b + (j - 4) // 2 + 1)
                    wh = j // 4
                    for q in range(4):
                        c16 = 4 * (j % 4) + q
                        last = pe.transpose(bank[2 + j % 4][:, P * q:P * (q + 1)],
                                            hrow[:, c16 * W + wh * P:c16 * W + (wh + 1) * P], ident[:])
                    last.then_inc(turn_done, 1)
                pe.wait_ge(turn_act, 4 * (b + 1))
                pe.wait_ge(turn_dve, 4 * (b + 1))
                for k in range(KP):
                    rows = [(0, k)] + [(1, KP - 1 + k)] * (k > 0)
                    todo = [(wh, sc, m) for wh in range(2) for sc, m in rows]
                    for n, (wh, sc, m) in enumerate(todo):
                        for ri in range(2):
                            last = pe.matmul(bank[6][ri * C:(ri + 1) * C, 2 * KX * k:2 * KX * (k + 1)],
                                             hcol[:, (wh * ROWS + m) * C:(wh * ROWS + m + 1) * C],
                                             dft_w[:, wh, 2 * sc + ri, :],
                                             start=n == 0, stop=n == len(todo) - 1, tile_position=(0, ri * C))
                last.then_inc(w_done, 1)
                pe.wait_ge(modes_in, b + 1)

            with pe.Fori(0, NB) as b:
                forward(b)

            def turn_kernels(q, first=False):
                q, buf = q
                pe.wait_ge(k_neg, q + 1)
                for t in range(2):
                    for j in range(3):
                        if t == 0 and not first:
                            pe.wait_ge(kt_dve, 3 * q - 2 + j)
                        if t == 1:
                            pe.wait_ge(kt_act, 3 * q + j + 1)
                        for s in range(4 * j, min(4 * j + 4, 10)):
                            last = pe.transpose(bank[j][:, P * (s - 4 * j):P * (s - 4 * j + 1)],
                                                kbuf[buf][:, (3 * s + 1 - t) * C:(3 * s + 3 - t) * C], ident[:])
                        last.then_inc(kt_group, 1)

            def mix(q, k, minus):
                q, buf = q
                pe.wait_ge(kt_act, 3 * q + 3)
                pe.wait_ge(kt_dve, 3 * q + 3)
                if minus:
                    wait(pe, yminus_in, k - 1)
                else:
                    wait(pe, ysum_in, k)
                for kx in range(KX):
                    at = ((minus * KP + k) * KX + kx) * NB
                    last = pe.matmul(bank[3 + minus][:, kx * NB:(kx + 1) * NB],
                                     lbuf[buf][:, kx * P:(kx + 1) * P],
                                     modes[:, bass.ds(at, NB)], start=True, stop=True)
                last.then_inc(mix_done, 1)

            def spread(k):
                pe.wait_ge(y3_in, k + 1)
                pe.wait_ge(y1_in, k + 1)
                zero = isinstance(k, int) and k == 0
                for i in range(4 if zero else 8):
                    row, ps, bh = i // 4, i // 2 % 2, i % 2
                    wait(pe, s_dve if bh else s_act, i // 2 if zero else 4 * k - 2 + i // 2)
                    for b in range(BH):
                        o = row * RB + (bh * BH + b) * YCOLS + ps * 2 * KX
                        last = pe.matmul(bank[5 + bh][0:SROWS, b * C:(b + 1) * C], ypart[:, o:o + SROWS],
                                         sel[:], start=True, stop=True)
                    last.then_inc(s_done, 1)

            def step(k):
                turn_kernels((2 * k, 0))
                mix((2 * k - 1, 1), k, 0)
                spread(k - 1)
                turn_kernels((2 * k + 1, 1))
                mix((2 * k, 0), k, 1)

            turn_kernels((0, 0), first=True)
            turn_kernels((1, 1))
            mix((0, 0), 0, 0)
            step(1)
            with pe.Fori(2, 10) as k:
                step(k)
            mix((19, 1), 10, 1)
            spread(9)
            spread(10)

            def turn_x(U, u):
                if u % 4 == 0:
                    j = u // 4
                    n, s = U
                    pe.wait_ge(x_in[j % SLOTS], 16 * (2 * NB + 2 * n + j // SLOTS + 1))
                n, s = U
                wait(pe, xt_in, n * UNITS + u - 1)
                base = (u // 4) % SLOTS * TILE + (u % 4) * UNIT
                for q in range(4):
                    last = pe.transpose(bank[u % 2][:, P * q:P * (q + 1)],
                                        ring[:, base + P * q:base + P * (q + 1)], ident[:])
                last.then_inc(xt_done, 1)

            def inverse_w(b, half, v):
                n = (2 * b + half) * GROUPS + v
                wait(pe, brest_in, n - 1)
                pe.wait_ge(copies_in, n + 1)
                for c in range(4):
                    for ps in range(2):
                        at = (2 * c + ps) * BROWS
                        last = pe.matmul(bank[6 + v % 2][0:BROWS, c * P:(c + 1) * P],
                                         copies[:, v % 2, at:at + BROWS],
                                         inv_w[:, ps, half * P:(half + 1) * P], start=ps == 0, stop=ps == 1)
                last.then_inc(iw_done, 1)

            def sum_unit(b, u):
                j = u // 4
                hh, wq, half = j % 2, j // 2, j // 8
                if u % (UNITS // 2) == 0:
                    pe.wait_ge(b_in, (2 * b + half + 1) * GROUPS)
                wait(pe, added, b * UNITS + u - 3)
                at = (wq % 4 * TILE_W * C) + (u % 4) * UNIT
                o = bank[2 + u % 4]
                pe.matmul(o[:], inv_h[:, hh, :], bst[half][:, at:at + UNIT], start=True, stop=False)
                pe.wait_ge(xt_in, b * UNITS + u + 1)
                for q in range(4):
                    last = pe.matmul(o[:, P * q:P * (q + 1)], xt[:, u % 2, P * q:P * (q + 1)], w_blk[:],
                                     start=False, stop=q == 3)
                last.then_inc(unit_done, 1)

            def inverse(b, last):
                for u in range(UNITS):
                    if u + 1 < UNITS:
                        turn_x((b, 0), u + 1)
                    elif not last:
                        turn_x((b + 1, 0), 0)
                    if u % 2 == 0:
                        v = u // 2 % GROUPS
                        if u < UNITS // 2:
                            inverse_w(b, 1, v)
                        elif not last:
                            inverse_w(b + 1, 0, v)
                    sum_unit(b, u)

            for v in range(GROUPS):
                inverse_w(0, 0, v)
            turn_x((0, 0), 0)
            inverse(0, False)
            with pe.Fori(1, NB - 1) as b:
                inverse(b, False)
            inverse(NB - 1, True)

        def put_turned(copy, j):
            wh = j // 4
            src = bank[2 + j % 4][:].rearrange("p (q g m) -> p q g m", q=4, g=4)[:, :, :, 0:ROWS]
            return copy(sub(hcol, wh * ROWS * C + 4 * (j % 4), [[1, 4], [16, 4], [C, ROWS]]), src)

        def put_kernels(copy, t, j, buf):
            n = min(4, 10 - 4 * j)
            src = bank[j][:, 0:n * P].rearrange("p (s m i) -> p s m i", m=2, i=C)
            return copy(sub(lbuf[buf], 4 * j * 2 * P + t * C, [[2 * P, n], [P, 2], [1, C]]), src)

        def put_spread(copy, i, k):
            row, ps, bh = i // 4, i // 2 % 2, i % 2
            kyr = k + 10 * row
            src = bank[5 + bh][0:SROWS, 0:BH * C].rearrange("p (b c) -> p b c", c=C)
            return copy(sub(spec[0:SROWS, :], kyr + bh * BH * SB + ps * ROWS, [[SB, BH], [2 * ROWS, C]]), src)

        def halves(rows, rep):
            for ri in range(2):
                yield (slice(ri * C, (ri + 1) * C),
                       sub(ypart[ri * C:(ri + 1) * C, :], rep * 2 * KX + ri * KX,
                           [[RB + (1 - 2 * ri) * KX, rows], [YCOLS, NB], [1, KX]]))

        def by_image(buf, part_slice, rows):
            return sub(buf[part_slice, :], 0, [[KX * NB, rows], [1, NB], [NB, KX]])

        @block.scalar
        def _(act):
            act.wait_ge(w_turned, 1)
            act.copy(w_blk[:], bank[7][:, 0:P]).then_inc(w_ready, 1)

            def forward(b):
                for t in range(TILES // 2):
                    act.wait_ge(h_done, b * (TILES // 2) + t + 1)
                    act.copy(sub(hrow, t * TILE_W, [[1, TILE_W], [W, 16]]),
                             bank[t % 2][:].rearrange("p (w c) -> p w c", c=16)).then_inc(h_evac, 1)
                for j in range(1, 8, 2):
                    act.wait_ge(turn_done, 8 * b + j + 1)
                    put_turned(act.copy, j).then_inc(turn_act, 1)
                act.wait_ge(w_done, b + 1)
                src = bank[6][:, 0:KP * 2 * KX].rearrange("p (k s x) -> p k s x", s=2, x=KX)
                dst = modes.rearrange("p (s k x b) -> p k s x b", s=2, k=KP, b=NB)[:, :, :, :, bass.ds(b, 1)]
                for s in range(2):
                    last = act.copy(dst[:, :, s].rearrange("p k x b -> p k (x b)"), src[:, :, s])
                last.then_inc(modes_in, 1)

            with act.Fori(0, NB) as b:
                forward(b)

            def kernels(q, buf):
                wait(act, mix_done, q - 1)
                for j in range(3):
                    act.wait_ge(kt_group, 6 * q + j + 1)
                    put_kernels(act.copy, 0, j, buf).then_inc(kt_act, 1)

            def minus(k, mixed):
                act.wait_ge(mix_done, mixed)
                act.wait_ge(ysum_in, k)
                act.copy(yminus, bank[4][:, 0:KX * NB]).then_inc(yminus_in, 1)

            def parts(k, rows, s_before):
                act.wait_ge(ysum_in, k + 1)
                wait(act, s_done, s_before)
                for rep in (1, 3):
                    for ps, dst in halves(rows, rep):
                        last = act.copy(dst, by_image(ysum, ps, rows))
                last.then_inc(y1_in, 1)
                act.wait_ge(yrest_in, k + 1)
                for ps, dst in halves(rows, 2):
                    last = act.copy(dst, by_image(yrest, ps, rows))
                last.then_inc(y2_in, 1)
                for i in range(0, 4 * rows, 2):
                    act.wait_ge(s_done, s_before + i + 1)
                    put_spread(act.copy, i, k).then_inc(s_act, 1)

            act.wait_ge(zeroed, 1)
            kernels(0, 0)
            kernels(1, 1)
            kernels(2, 0)
            parts(0, 1, 0)
            kernels(3, 1)
            with act.Fori(2, 10) as k:
                minus(k - 1, 2 * k - 1)
                kernels(2 * k, 0)
                parts(k - 1, 2, 8 * k - 12)
                kernels(2 * k + 1, 1)
            minus(9, 19)
            parts(9, 2, 8 * 9 - 4)
            minus(10, 20)
            parts(10, 2, 8 * 10 - 4)

            def take_x(b, u):
                act.wait_ge(xt_done, b * UNITS + u + 1)
                wait(act, unit_done, b * UNITS + u - 1)
                act.copy(xt[:, u % 2, :], bank[u % 2][:]).then_inc(xt_in, 1)

            def first_part(b, half, v):
                n = (2 * b + half) * GROUPS + v
                act.wait_ge(iw_done, n + 1)
                wait(act, brest_in, n - 1)
                act.copy(b1[:, v % 2, :], bank[6 + v % 2][0:BROWS, :]).then_inc(b1_in, 1)

            def second_part(b, half, v):
                n = (2 * b + half) * GROUPS + v
                act.wait_ge(brest_in, n + 1)
                wait(act, b_in, n - 1)
                act.copy(b2[:, v % 2, :], brest[:, v % 2, :]).then_inc(b2_in, 1)

            def inverse(b, last):
                for u in range(UNITS):
                    if u + 1 < UNITS:
                        take_x(b, u + 1)
                    elif not last:
                        take_x(b + 1, 0)
                    v = u // 2 % GROUPS
                    step = second_part if u % 2 else first_part
                    if u < UNITS // 2:
                        step(b, 1, v)
                    elif not last:
                        step(b + 1, 0, v)

            first_part(0, 0, 0)
            for v in range(GROUPS):
                if v + 1 < GROUPS:
                    first_part(0, 0, v + 1)
                second_part(0, 0, v)
            take_x(0, 0)
            inverse(0, False)
            with act.Fori(1, NB - 1) as b:
                inverse(b, False)
            inverse(NB - 1, True)

        @block.vector
        def _(dve):
            def exact_copy(dst, src):
                return dve.tensor_scalar(dst, src, 1.0, None, ALU.mult)

            def forward(b):
                for j in range(0, 8, 2):
                    dve.wait_ge(turn_done, 8 * b + j + 1)
                    put_turned(dve.tensor_copy, j).then_inc(turn_dve, 1)
                dve.wait_ge(w_done, b + 1)

            with dve.Fori(0, NB) as b:
                forward(b)

            def kernels(q, buf):
                wait(dve, mix_done, q - 1)
                for j in range(3):
                    dve.wait_ge(kt_group, 6 * q + 3 + j + 1)
                    put_kernels(dve.tensor_copy, 1, j, buf).then_inc(kt_dve, 1)

            yk = bank[3][:, 0:KX * NB]
            row = [ysum[:, r * KX * NB:(r + 1) * KX * NB] for r in range(2)]

            def combine(k):
                if isinstance(k, int) and k == 0:
                    dve.wait_ge(mix_done, 1)
                    dve.tensor_copy(row[0], yk).then_inc(ysum_in, 1)
                elif isinstance(k, int) and k == 10:
                    dve.wait_ge(yminus_in, 10)
                    dve.tensor_copy(row[0], yminus)
                    dve.tensor_scalar(row[1][0:C, :], yminus[0:C, :], -1.0, None, ALU.mult)
                    dve.tensor_copy(row[1][C:P, :], yminus[C:P, :]).then_inc(ysum_in, 1)
                else:
                    dve.wait_ge(mix_done, 2 * k)
                    dve.wait_ge(yminus_in, k)
                    dve.tensor_tensor(row[0], yk, yminus, ALU.add)
                    dve.tensor_tensor(row[1][0:C, :], yk[0:C, :], yminus[0:C, :], ALU.subtract)
                    dve.tensor_tensor(row[1][C:P, :], yminus[C:P, :], yk[C:P, :],
                                      ALU.subtract).then_inc(ysum_in, 1)

            def parts(k, rows, s_before):
                dve.wait_ge(y1_in, k + 1)
                for ps, y1 in halves(rows, 1):
                    last = dve.tensor_tensor(by_image(yrest, ps, rows), by_image(ysum, ps, rows), y1, ALU.subtract)
                last.then_inc(yrest_in, 1)
                dve.wait_ge(y2_in, k + 1)
                for (ps, y2), (_, y3) in zip(halves(rows, 2), halves(rows, 0)):
                    last = dve.tensor_tensor(y3, by_image(yrest, ps, rows), y2, ALU.subtract)
                last.then_inc(y3_in, 1)
                for i in range(1, 4 * rows, 2):
                    dve.wait_ge(s_done, s_before + i + 1)
                    put_spread(exact_copy, i, k).then_inc(s_dve, 1)

            kernels(0, 0)
            kernels(1, 1)
            combine(0)
            kernels(2, 0)
            parts(0, 1, 0)
            kernels(3, 1)
            with dve.Fori(2, 10) as k:
                combine(k - 1)
                kernels(2 * k, 0)
                parts(k - 1, 2, 8 * k - 12)
                kernels(2 * k + 1, 1)
            combine(9)
            parts(9, 2, 8 * 9 - 4)
            combine(10)
            parts(10, 2, 8 * 10 - 4)

            def copy_six(b, half, v):
                n = (2 * b + half) * GROUPS + v
                wait(dve, iw_done, n - 1)
                src = sub(spec[0:SROWS, :], b * SB + 8 * v * ROWS, [[ROWS, 8], [0, 6], [1, ROWS]])
                exact_copy(copies[:, v % 2, :].rearrange("p (a r k) -> p a r k", r=6, k=ROWS),
                           src).then_inc(copies_in, 1)

            def rest(b, half, v):
                n = (2 * b + half) * GROUPS + v
                dve.wait_ge(b1_in, n + 1)
                wait(dve, b_in, n - 1)
                dve.scalar_tensor_tensor(brest[:, v % 2, :], b1[:, v % 2, :], part[:, 0:1],
                                         bank[6 + v % 2][0:BROWS, :], ALU.mult, ALU.add).then_inc(brest_in, 1)

            def row_part(b, half, v):
                n = (2 * b + half) * GROUPS + v
                dve.wait_ge(b2_in, n + 1)
                dve.scalar_tensor_tensor(sub(bst[half], 4 * v, [[1, 4], [C, P]]),
                                         b2[:, v % 2, :].rearrange("p (c w) -> p c w", c=4), part[:, 1:2],
                                         brest[:, v % 2, :].rearrange("p (c w) -> p c w", c=4),
                                         ALU.mult, ALU.add).then_inc(b_in, 1)

            def add_x(b, u):
                j = u // 4
                at = j % SLOTS * TILE + (u % 4) * UNIT
                dve.wait_ge(unit_done, b * UNITS + u + 1)
                dve.tensor_tensor(ring[:, at:at + UNIT], bank[2 + u % 4][:], ring[:, at:at + UNIT],
                                  ALU.add).then_inc(added, 1)

            def inverse(b, last):
                for u in range(UNITS):
                    v = u // 2 % GROUPS
                    step = row_part if u % 2 else rest
                    if u < UNITS // 2:
                        step(b, 1, v)
                    elif not last:
                        step(b + 1, 0, v)
                    if u % 2 == 0:
                        ahead = u // 2 + 2 + GROUPS
                        if ahead < 2 * GROUPS:
                            copy_six(b, 1, ahead % GROUPS)
                        elif not last:
                            copy_six(b + 1, ahead // GROUPS - 2, ahead % GROUPS)
                    add_x(b, u)

            dve.wait_ge(s_act, 4 * 10 + 2)
            dve.wait_ge(s_dve, 4 * 10 + 2)
            copy_six(0, 0, 0)
            copy_six(0, 0, 1)
            rest(0, 0, 0)
            for v in range(GROUPS):
                if v + 2 < GROUPS:
                    copy_six(0, 0, v + 2)
                if v + 1 < GROUPS:
                    rest(0, 0, v + 1)
                row_part(0, 0, v)
            copy_six(0, 1, 0)
            copy_six(0, 1, 1)
            inverse(0, False)
            with dve.Fori(1, NB - 1) as b:
                inverse(b, False)
            inverse(NB - 1, True)


def tables():
    import numpy as np

    def parts(a):
        a = a.astype(np.float32)
        p = []
        for _ in range(3):
            p.append(((a.view(np.uint32) + 0x8000) & 0xFFFF0000).view(np.float32))
            a = a - p[-1]
        return p

    def angle(f, n):
        return 2 * np.pi * (np.outer(f, n) % 256) / 256

    n = np.arange(256)
    k, kx = np.arange(KP), np.arange(KX)
    row_h = np.concatenate([np.cos(angle(k, n)), np.sin(angle(k[1:], n))])
    t_h = np.zeros((P, 2, 32), np.float32)
    t_h[:, :, 0:ROWS] = row_h.reshape(ROWS, 2, P).transpose(2, 1, 0)
    c, s = np.cos(angle(kx, n)), np.sin(angle(kx, n))
    v = np.stack([np.stack([c, c]), np.stack([-s, -s]), np.stack([-s, s]), np.stack([-c, c])])
    t_w = v.reshape(4, 2 * KX, 2, P).transpose(3, 2, 0, 1).astype(np.float32)
    weight = np.where(kx == 0, 1.0, 2.0)[:, None] / (H * W)
    g = parts(np.concatenate([weight * c, -weight * s]))
    t_iw = np.stack([np.concatenate([g[0], g[0], g[0]]), np.concatenate([g[1], g[1], g[2]])], 1)
    f = parts(row_h)
    t_ih = np.concatenate([f[0], f[0], f[0], f[1], f[1], f[2]]).reshape(BROWS, 2, P)
    p = np.array([[0, 0], [-1, 0], [-1, -1], [0, 0], [-1, 0], [0, 0]], np.float32)
    t_part = np.repeat(p, ROWS, axis=0)
    t_sel = np.concatenate([np.eye(C), np.eye(C)]).astype(np.float32)
    return dict(t_h=t_h, t_w=t_w, t_id=np.eye(P, dtype=np.float32), t_sel=t_sel, t_iw=t_iw, t_ih=t_ih, t_part=t_part)


def kernel(x, L0_conv_kernel_real, L0_conv_kernel_imag, L0_conv_w_lin):
    import numpy as np
    import concourse.bacc as bacc
    from concourse.bass_utils import run_bass_kernel_spmd

    nc = bacc.Bacc("TRN2", target_bir_lowering=False, num_devices=1)
    given = dict(x=x, k_re=L0_conv_kernel_real, k_im=L0_conv_kernel_imag, w_lin=L0_conv_w_lin)
    arrays, args = {}, {}
    for name, a in {**given, **tables()}.items():
        a = np.ascontiguousarray(a)
        arrays[f"in_{name}"] = a
        args[name] = nc.dram_tensor(f"in_{name}", a.shape, mybir.dt.from_np(a.dtype), kind="ExternalInput").ap()
    args["out"] = nc.dram_tensor("out_y", args["x"].shape, F32, kind="ExternalOutput").ap()
    spectral_conv(nc, **args)
    r = run_bass_kernel_spmd(nc, [arrays], core_ids=[0])
    return r.results[0]["out_y"]
```

```python
from contextlib import ExitStack

import concourse.bass as bass
from concourse import mybir

F32 = mybir.dt.float32
BF16 = mybir.dt.bfloat16
ALU = mybir.AluOpType

P = 128
H = W = 256
C = 64
KX = 20
KP = 11
ROWS = 2 * KP - 1
MODES_Y = 20
TILE_W = 32
TILE = TILE_W * C
SLOTS = 8
TILES = 2 * W // TILE_W
UNIT = 512
UNITS = TILES * TILE // UNIT
GROUPS = 16
BROWS = 6 * ROWS
SROWS = 3 * 2 * KX
KH = KX // 4
PAIRS = (KH + 1) // 2
YCOLS = 4 * 2 * KX


def wait(eng, sem, value):
    if not (isinstance(value, int) and value <= 0):
        eng.wait_ge(sem, value)


def sub(base, offset, dims):
    return bass.AP(base.tensor, base.offset + offset, [list(base.ap[0])] + dims)


def spectral_conv(nc, x, k_re, k_im, w_lin, t_h, t_w, t_id, t_sel, t_iw, t_ih, t_part, out):
    NB = x.shape[0]
    BH = NB // 2
    RB = NB * YCOLS
    SB = 2 * C * ROWS
    with ExitStack() as ctx:
        def sb(name, shape, dt):
            return ctx.enter_context(nc.sbuf_tensor(name, shape, dt))

        def sem(name):
            return ctx.enter_context(nc.semaphore(name))

        bank = [ctx.enter_context(nc.psum_tensor(f"bank{i}", [P, UNIT], F32)) for i in range(8)]

        dft_h = sb("dft_h", [P, 2, 32], F32)
        dft_w = sb("dft_w", [P, 2, 4, 2 * KX], F32)
        ident = sb("ident", [P, P], F32)
        sel = sb("sel", [P, C], BF16)
        inv_w = sb("inv_w", [SROWS, 2, W], BF16)
        inv_h = sb("inv_h", [BROWS, 2, P], BF16)
        part = sb("part", [BROWS, 2], F32)
        w_nat = sb("w_nat", [P, P], F32)
        w_blk = sb("w_blk", [P, P], F32)

        ring = sb("ring", [P, SLOTS * TILE], F32)
        KN = KX * C * C // P
        offset = 0

        def stage_two(words):
            nonlocal offset
            offset += words
            assert offset <= SLOTS * TILE
            return ring[:, offset - words:offset]

        YW = PAIRS * P
        kbuf = [stage_two(2 * KN) for _ in range(2)]
        lbuf = [stage_two(KX * C) for _ in range(2)]
        mstat = [stage_two(KX * 2 * NB) for _ in range(2)]
        mixed = [stage_two(YW) for _ in range(2)]
        ypart = [stage_two(RB).bitcast(BF16) for _ in range(2)]
        yplus = stage_two(YW)
        yminus = stage_two(YW)
        ysum = stage_two(2 * YW)

        half_buf = sb("half_buf", [P, 2 * P * C], BF16)
        bst = [half_buf[0:BROWS, h * P * C:(h + 1) * P * C] for h in range(2)]
        modes = half_buf[:, 0:2 * 2 * KP * KX * NB].bitcast(F32)

        spec = sb("spec", [P, max(16, NB) * SB], BF16)
        hrow = spec[:, 0:2 * 16 * W].bitcast(F32)
        hcol = spec[:, 2 * 16 * W:2 * 16 * W + 4 * ROWS * C].bitcast(F32)

        xt = sb("xt", [P, 2, UNIT], F32)
        yrest = xt[:].rearrange("p a b -> p (a b)")[:, 0:2 * YW]
        copies = sb("copies", [SROWS, 2, 8 * BROWS], BF16)
        b1 = sb("b1", [BROWS, 2, UNIT], BF16)
        brest = sb("brest", [BROWS, 2, UNIT], F32)
        b2 = sb("b2", [BROWS, 2, UNIT], BF16)

        tables_in = sem("tables_in")
        cast_in = sem("cast_in")
        w_zeroed = sem("w_zeroed")
        w_turned = sem("w_turned")
        w_ready = sem("w_ready")
        x_in = [sem(f"x_in{s}") for s in range(SLOTS)]
        h_done = sem("h_done")
        h_evac = sem("h_evac")
        turn_done = sem("turn_done")
        turn_act = sem("turn_act")
        turn_dve = sem("turn_dve")
        w_done = sem("w_done")
        modes_in = sem("modes_in")
        k_in = [sem(f"k_in{q}") for q in range(2)]
        kt_group = sem("kt_group")
        kt_act = sem("kt_act")
        kt_dve = sem("kt_dve")
        mstat_act = sem("mstat_act")
        mstat_dve = sem("mstat_dve")
        mix_done = sem("mix_done")
        mixed_in = sem("mixed_in")
        y_turned = sem("y_turned")
        y_in = sem("y_in")
        ysum_in = sem("ysum_in")
        y1_in = sem("y1_in")
        y1_again = sem("y1_again")
        yrest_in = sem("yrest_in")
        y2_in = sem("y2_in")
        y3_in = sem("y3_in")
        zeroed = sem("zeroed")
        s_done = sem("s_done")
        s_act = sem("s_act")
        s_dve = sem("s_dve")
        xt_done = sem("xt_done")
        xt_in = sem("xt_in")
        unit_done = sem("unit_done")
        added = sem("added")
        stored = [sem(f"stored{s}") for s in range(SLOTS)]
        copies_in = sem("copies_in")
        iw_done = sem("iw_done")
        b1_in = sem("b1_in")
        brest_in = sem("brest_in")
        b2_in = sem("b2_in")
        b_in = sem("b_in")

        def slot(s):
            return ring[:, s * TILE:(s + 1) * TILE]

        def x_tile(t, b, j):
            hh, wq = j % 2, j // 2
            return t[bass.ds(b, 1), hh * P:(hh + 1) * P, wq * TILE_W:(wq + 1) * TILE_W, :].rearrange(
                "b h w c -> h (b w c)")

        def put_turned(copy, j):
            wh = j // 4
            src = bank[2 + j % 4][:].rearrange("p (q g m) -> p q g m", q=4, g=4)[:, :, :, 0:ROWS]
            return copy(sub(hcol, wh * ROWS * C + 4 * (j % 4), [[1, 4], [16, 4], [C, ROWS]]), src)

        K_BANKS, MIX_BANKS, Y_BANK = (0, 1, 5), (2, 4), 3

        def put_kernels(copy, j, buf):
            n = min(UNIT, KX * C - UNIT * j)
            return copy(lbuf[buf][:, UNIT * j:UNIT * j + n], bank[K_BANKS[j]][:, 0:n])

        def put_spread(copy, i, k):
            row, ps, bh = i // 4, i // 2 % 2, i % 2
            kyr = k + 10 * row
            src = bank[6 + bh][0:SROWS, 0:BH * C].rearrange("p (b c) -> p b c", c=C)
            return copy(sub(spec[0:SROWS, :], kyr + bh * BH * SB + ps * ROWS, [[SB, BH], [2 * ROWS, C]]), src)

        def stationary(copy, q, s, k, ri, half, ro):
            buf = q[1]
            src = modes[ri * C:(ri + 1) * C, bass.ds((s * KP + k) * KX * NB, KX * NB)]
            dst = mstat[buf].rearrange("p (x r b) -> p x r b", r=2, b=NB)[half * C:(half + 1) * C, :, ro]
            return copy(dst, src.rearrange("p (x b) -> p x b", b=NB))

        def y_to(par, h, rep, rows):
            n = 8 * (PAIRS if h == 0 else KH // 2)
            return sub(ypart[par][h * C:(h + 1) * C, :], rep * 2 * KX + h * 8 * PAIRS,
                       [[YCOLS, rows * NB], [1, n]]) if rows == 1 else sub(
                ypart[par][h * C:(h + 1) * C, :], rep * 2 * KX + h * 8 * PAIRS, [[RB, 2], [YCOLS, NB], [1, n]])

        def y_from(buf, h, rows):
            n = 8 * (PAIRS if h == 0 else KH // 2)
            dims = [[1, NB], [NB, n]]
            return sub(buf[h * C:(h + 1) * C, :], 0, dims if rows == 1 else [[YW, 2]] + dims)

        block = ctx.enter_context(nc.Block())

        @block.sync
        def _(sp):
            def load(b, j):
                sp.dma_start(slot(j % SLOTS), x_tile(x, b, j)).then_inc(x_in[j % SLOTS], 16)

            for dst, src in ((dft_h, t_h), (ident, t_id)):
                sp.dma_start(dst[:], src).then_inc(tables_in, 16)
            for j in range(SLOTS):
                load(0, j)
            for dst, src in ((dft_w, t_w), (part, t_part)):
                sp.dma_start(dst[:], src).then_inc(tables_in, 16)
            sp.wait_ge(w_zeroed, 1)
            for e in range(2):
                sp.dma_start(w_nat[e * C:(e + 1) * C, e * C:(e + 1) * C], w_lin).then_inc(tables_in, 16)

            def forward(b, last):
                for t in range(TILES // 2):
                    later = t + SLOTS // 2
                    if last and later >= TILES // 2:
                        break
                    sp.wait_ge(h_done, b * (TILES // 2) + t + 1)
                    for hh in range(2):
                        if later < TILES // 2:
                            load(b, 2 * later + hh)
                        else:
                            load(b + 1, 2 * (later - TILES // 2) + hh)

            with sp.Fori(0, NB - 1) as b:
                forward(b, False)
            forward(NB - 1, True)

            def kernels(q, row):
                for t, src in enumerate((k_re, k_im)):
                    flat = src[bass.ds(row, 1)].rearrange("x y i j -> (x y i) j").rearrange("(s p) j -> p s j", p=P)
                    dst = kbuf[q].rearrange("p (s t j) -> p s t j", t=2, j=C)[:, :, t, :]
                    sp.dma_start(dst, flat).then_inc(k_in[q], 16)

            sp.wait_ge(h_done, NB * (TILES // 2))
            kernels(0, 10)
            kernels(1, 11)
            sp.wait_ge(kt_group, 3)
            kernels(0, 9)
            with sp.Fori(2, 10) as k:
                minus_k = sp.snap(k * -1 + 10)
                sp.wait_ge(kt_group, 6 * k - 6)
                kernels(1, 10 + k)
                sp.wait_ge(kt_group, 6 * k - 3)
                kernels(0, minus_k)
            sp.wait_ge(kt_group, 3 * 18)
            kernels(1, 0)

            sp.wait_ge(s_done, 8 * 10 + 4)
            for j in range(SLOTS):
                load(0, j)

            def inverse(b, first, last):
                for j in range(TILES):
                    sp.wait_ge(added, b * UNITS + 4 * (j + 1))
                    sp.dma_start(x_tile(out, b, j), slot(j % SLOTS)).then_inc(stored[j % SLOTS], 16)
                    if (first and j == 0) or (last and j + SLOTS - 1 >= TILES):
                        continue
                    before = (j - 1) % SLOTS
                    n = 2 * b + (j - 1) // SLOTS + 1
                    sp.wait_ge(stored[before], 16 * n)
                    j2 = j + SLOTS - 1
                    load(b if j2 < TILES else b + 1, j2 % TILES)

            inverse(0, True, False)
            with sp.Fori(1, NB - 1) as b:
                inverse(b, False, False)
            inverse(NB - 1, False, True)
            for s in range(SLOTS):
                sp.wait_ge(stored[s], 16 * 2 * NB)

        @block.gpsimd
        def _(pool):
            pool.memset(w_nat[:], 0.0).then_inc(w_zeroed, 1)
            for dst, src in ((sel, t_sel), (inv_w, t_iw), (inv_h, t_ih)):
                pool.dma_start(dst[:], src).then_inc(cast_in, 16)
            pool.wait_ge(h_done, NB * (TILES // 2))
            for q in range(2):
                pool.memset(mixed[q][:, KH * C:], 0.0).then_inc(zeroed, 1)

            for par in range(2):
                pool.memset(ypart[par], 0.0).then_inc(zeroed, 1)

        @block.tensor
        def _(pe):
            pe.wait_ge(tables_in, 6 * 16)
            pe.wait_ge(cast_in, 3 * 16)
            pe.transpose(bank[7][:, 0:P], w_nat[:], ident[:]).then_inc(w_turned, 1)

            def forward(b):
                for t in range(TILES // 2):
                    for hh in range(2):
                        s = 2 * (t % (SLOTS // 2)) + hh
                        pe.wait_ge(x_in[s], 16 * (2 * b + t // (SLOTS // 2) + 1))
                    if t > 1:
                        pe.wait_ge(h_evac, b * (TILES // 2) + t - 1)
                    for hh in range(2):
                        tile = slot(2 * (t % (SLOTS // 2)) + hh).rearrange("p (w c) -> p w c", c=C)
                        for g in range(4):
                            last = pe.matmul(bank[t % 2][32 * g:32 * g + 32, :], dft_h[:, hh, :],
                                             tile[:, :, 16 * g:16 * g + 16], start=hh == 0, stop=hh == 1,
                                             tile_position=(0, 32 * g))
                    last.then_inc(h_done, 1)
                pe.wait_ge(h_evac, (b + 1) * (TILES // 2))
                for j in range(8):
                    if j >= 4:
                        pe.wait_ge(turn_act if j % 2 else turn_dve, 4 * b + (j - 4) // 2 + 1)
                    wh = j // 4
                    for q in range(4):
                        c16 = 4 * (j % 4) + q
                        last = pe.transpose(bank[2 + j % 4][:, P * q:P * (q + 1)],
                                            hrow[:, c16 * W + wh * P:c16 * W + (wh + 1) * P], ident[:])
                    last.then_inc(turn_done, 1)
                pe.wait_ge(turn_act, 4 * (b + 1))
                pe.wait_ge(turn_dve, 4 * (b + 1))
                for k in range(KP):
                    rows = [(0, k)] + [(1, KP - 1 + k)] * (k > 0)
                    todo = [(wh, sc, m) for wh in range(2) for sc, m in rows]
                    for n, (wh, sc, m) in enumerate(todo):
                        for ri in range(2):
                            last = pe.matmul(bank[6][ri * C:(ri + 1) * C, 2 * KX * k:2 * KX * (k + 1)],
                                             hcol[:, (wh * ROWS + m) * C:(wh * ROWS + m + 1) * C],
                                             dft_w[:, wh, 2 * sc + ri, :],
                                             start=n == 0, stop=n == len(todo) - 1, tile_position=(0, ri * C))
                last.then_inc(w_done, 1)
                pe.wait_ge(modes_in, b + 1)

            with pe.Fori(0, NB) as b:
                forward(b)

            def turn_kernels(q, kin, first=False):
                q, buf = q
                pe.wait_ge(k_in[buf], 32 * kin)
                for j in range(3):
                    if not first:
                        pe.wait_ge(*((kt_act, 2 * q - 1), (kt_dve, q), (kt_act, 2 * q))[j])
                    for s in range(4 * j, min(4 * j + 4, KX // 2)):
                        last = pe.transpose(bank[K_BANKS[j]][:, P * (s - 4 * j):P * (s - 4 * j + 1)],
                                            kbuf[buf][:, s * P:(s + 1) * P], ident[:])
                    last.then_inc(kt_group, 1)

            def mix(q):
                q, buf = q
                pe.wait_ge(kt_act, 2 * q + 2)
                pe.wait_ge(kt_dve, q + 1)
                pe.wait_ge(mstat_act, q + 1)
                pe.wait_ge(mstat_dve, q + 1)
                wait(pe, mixed_in, q - 1)
                for kx in range(KX):
                    g, kh = kx % 4, kx // 4
                    last = pe.matmul(bank[MIX_BANKS[buf]][32 * g:32 * g + 2 * NB, kh * C:(kh + 1) * C],
                                     mstat[buf][:, kx * 2 * NB:(kx + 1) * 2 * NB],
                                     lbuf[buf][:, kx * C:(kx + 1) * C],
                                     start=True, stop=True, tile_position=(0, 32 * g))
                last.then_inc(mix_done, 1)

            def turn_mixed(q):
                q, buf = q
                pe.wait_ge(mixed_in, q + 1)
                wait(pe, y_in, q)
                for pair in range(PAIRS):
                    last = pe.transpose(bank[Y_BANK][:, pair * P:(pair + 1) * P],
                                        mixed[buf][:, pair * P:(pair + 1) * P], ident[:])
                last.then_inc(y_turned, 1)

            def spread(k, par, row, only=False):
                if row == 0:
                    pe.wait_ge(y3_in, k + 1)
                    pe.wait_ge(y1_again, k + 1)
                for i in range(4 * row, 4 * row + 4):
                    ps, bh = i // 2 % 2, i % 2
                    wait(pe, s_dve if bh else s_act, i // 2 if only else 4 * k - 2 + i // 2)
                    for b in range(BH):
                        o = row * RB + (bh * BH + b) * YCOLS + ps * 2 * KX
                        last = pe.matmul(bank[6 + bh][0:SROWS, b * C:(b + 1) * C], ypart[par][:, o:o + SROWS],
                                         sel[:], start=True, stop=True)
                    last.then_inc(s_done, 1)

            def step(k, par):
                first, second = isinstance(k, int) and k == 1, isinstance(k, int) and k == 2
                turn_kernels((2 * k, 0), k + 1)
                turn_mixed((2 * k - 2, 0))
                if not first:
                    spread(k - 2, par, 0, only=second)
                mix((2 * k - 1, 1))
                turn_kernels((2 * k + 1, 1), k + 1)
                turn_mixed((2 * k - 1, 1))
                if not (first or second):
                    spread(k - 2, par, 1)
                mix((2 * k, 0))

            turn_kernels((0, 0), 1, first=True)
            turn_kernels((1, 1), 1)
            pe.wait_ge(zeroed, 4)
            mix((0, 0))
            step(1, 1)
            step(2, 0)
            with pe.Fori(0, 3) as i:
                step(2 * i + 3, 1)
                step(2 * i + 4, 0)
            step(9, 1)
            mix((19, 1))
            turn_mixed((18, 0))
            spread(8, 0, 0)
            spread(8, 0, 1)
            turn_mixed((19, 1))
            for k in (9, 10):
                spread(k, k % 2, 0)
                spread(k, k % 2, 1)

            def turn_x(U, u):
                if u % 4 == 0:
                    j = u // 4
                    n, s = U
                    pe.wait_ge(x_in[j % SLOTS], 16 * (2 * NB + 2 * n + j // SLOTS + 1))
                n, s = U
                wait(pe, xt_in, n * UNITS + u - 1)
                base = (u // 4) % SLOTS * TILE + (u % 4) * UNIT
                for q in range(4):
                    last = pe.transpose(bank[u % 2][:, P * q:P * (q + 1)],
                                        ring[:, base + P * q:base + P * (q + 1)], ident[:])
                last.then_inc(xt_done, 1)

            def inverse_w(b, half, v):
                n = (2 * b + half) * GROUPS + v
                wait(pe, brest_in, n - 1)
                pe.wait_ge(copies_in, n + 1)
                for c in range(4):
                    for ps in range(2):
                        at = (2 * c + ps) * BROWS
                        last = pe.matmul(bank[6 + v % 2][0:BROWS, c * P:(c + 1) * P],
                                         copies[:, v % 2, at:at + BROWS],
                                         inv_w[:, ps, half * P:(half + 1) * P], start=ps == 0, stop=ps == 1)
                last.then_inc(iw_done, 1)

            def sum_unit(b, u):
                j = u // 4
                hh, wq, half = j % 2, j // 2, j // 8
                if u % (UNITS // 2) == 0:
                    pe.wait_ge(b_in, (2 * b + half + 1) * GROUPS)
                wait(pe, added, b * UNITS + u - 3)
                at = (wq % 4 * TILE_W * C) + (u % 4) * UNIT
                o = bank[2 + u % 4]
                pe.matmul(o[:], inv_h[:, hh, :], bst[half][:, at:at + UNIT], start=True, stop=False)
                pe.wait_ge(xt_in, b * UNITS + u + 1)
                for q in range(4):
                    last = pe.matmul(o[:, P * q:P * (q + 1)], xt[:, u % 2, P * q:P * (q + 1)], w_blk[:],
                                     start=False, stop=q == 3)
                last.then_inc(unit_done, 1)

            def inverse(b, last):
                for u in range(UNITS):
                    if u + 1 < UNITS:
                        turn_x((b, 0), u + 1)
                    elif not last:
                        turn_x((b + 1, 0), 0)
                    if u % 2 == 0:
                        v = u // 2 % GROUPS
                        if u < UNITS // 2:
                            inverse_w(b, 1, v)
                        elif not last:
                            inverse_w(b + 1, 0, v)
                    sum_unit(b, u)

            for v in range(GROUPS):
                inverse_w(0, 0, v)
            turn_x((0, 0), 0)
            inverse(0, False)
            with pe.Fori(1, NB - 1) as b:
                inverse(b, False)
            inverse(NB - 1, True)

        @block.scalar
        def _(act):
            act.wait_ge(w_turned, 1)
            act.copy(w_blk[:], bank[7][:, 0:P]).then_inc(w_ready, 1)

            def forward(b):
                for t in range(TILES // 2):
                    act.wait_ge(h_done, b * (TILES // 2) + t + 1)
                    act.copy(sub(hrow, t * TILE_W, [[1, TILE_W], [W, 16]]),
                             bank[t % 2][:].rearrange("p (w c) -> p w c", c=16)).then_inc(h_evac, 1)
                for j in range(1, 8, 2):
                    act.wait_ge(turn_done, 8 * b + j + 1)
                    put_turned(act.copy, j).then_inc(turn_act, 1)
                act.wait_ge(w_done, b + 1)
                src = bank[6][:, 0:KP * 2 * KX].rearrange("p (k s x) -> p k s x", s=2, x=KX)
                dst = modes.rearrange("p (s k x b) -> p k s x b", s=2, k=KP, b=NB)[:, :, :, :, bass.ds(b, 1)]
                for s in range(2):
                    last = act.copy(dst[:, :, s].rearrange("p k x b -> p k (x b)"), src[:, :, s])
                last.then_inc(modes_in, 1)

            with act.Fori(0, NB) as b:
                forward(b)

            def kernels(q, buf):
                wait(act, mix_done, q - 1)
                for j in (0, 2):
                    act.wait_ge(kt_group, 3 * q + j + 1)
                    put_kernels(act.copy, j, buf).then_inc(kt_act, 1)

            def stationaries(q, s, k):
                wait(act, mix_done, q[0] - 1)
                stationary(act.copy, q, s, k, 0, 0, 0)
                stationary(act.copy, q, s, k, 1, 0, 1)
                stationary(act.copy, q, s, k, 0, 1, 1).then_inc(mstat_act, 1)

            def take_turned(q, dst, used):
                act.wait_ge(y_turned, q + 1)
                wait(act, ysum_in, used)
                act.copy(dst, bank[Y_BANK][:, 0:YW]).then_inc(y_in, 1)

            def first_part_of(k, par, h, rows):
                if h == 0:
                    act.wait_ge(ysum_in, k + 1)
                    wait(act, s_done, 8 * k - 12)
                last = act.copy(y_to(par, h, 1, rows), y_from(ysum, h, rows))
                if h == 1:
                    last.then_inc(y1_in, 1)

            def second_part_of(k, par, h, rows):
                if h == 0:
                    act.wait_ge(yrest_in, k + 1)
                last = act.copy(y_to(par, h, 2, rows), y_from(yrest, h, rows))
                if h == 1:
                    last.then_inc(y2_in, 1)

            def take_spread(k, i):
                act.wait_ge(s_done, (0 if isinstance(k, int) and k == 0 else 8 * k - 4) + i + 1)
                put_spread(act.copy, i, k).then_inc(s_act, 1)

            def step(k, par, minus_ten=False):
                first, second = isinstance(k, int) and k == 1, isinstance(k, int) and k == 2
                rows = 1 if first else 2
                kernels(2 * k, 0)
                take_turned(2 * k - 2, yplus if first else yminus, k - 1)
                if not first:
                    take_spread(0 if second else k - 2, 0)
                first_part_of(k - 1, 1 - par, 0, rows)
                if not first:
                    take_spread(0 if second else k - 2, 2)
                first_part_of(k - 1, 1 - par, 1, rows)
                stationaries((2 * k, 0), 1, k)
                kernels(2 * k + 1, 1)
                take_turned(2 * k - 1, yplus, k)
                second_part_of(k - 1, 1 - par, 0, rows)
                if not (first or second):
                    take_spread(k - 2, 4)
                second_part_of(k - 1, 1 - par, 1, rows)
                stationaries((2 * k + 1, 1), int(minus_ten), k + 1)
                if not (first or second):
                    take_spread(k - 2, 6)

            act.wait_ge(h_done, NB * (TILES // 2))
            act.wait_ge(modes_in, NB)
            stationaries((0, 0), 0, 0)
            stationaries((1, 1), 0, 1)
            kernels(0, 0)
            kernels(1, 1)
            act.wait_ge(zeroed, 4)
            step(1, 1)
            step(2, 0)
            with act.Fori(0, 3) as i:
                step(2 * i + 3, 1)
                step(2 * i + 4, 0)
            step(9, 1, minus_ten=True)
            take_turned(18, yminus, 9)
            take_spread(8, 0)
            take_spread(8, 2)
            first_part_of(9, 1, 0, 2)
            first_part_of(9, 1, 1, 2)
            take_spread(8, 4)
            take_spread(8, 6)
            take_turned(19, yminus, 10)
            second_part_of(9, 1, 0, 2)
            second_part_of(9, 1, 1, 2)
            first_part_of(10, 0, 0, 2)
            first_part_of(10, 0, 1, 2)
            take_spread(9, 0)
            take_spread(9, 2)
            second_part_of(10, 0, 0, 2)
            second_part_of(10, 0, 1, 2)
            take_spread(9, 4)
            take_spread(9, 6)
            for i in range(0, 8, 2):
                take_spread(10, i)

            def take_x(b, u):
                act.wait_ge(xt_done, b * UNITS + u + 1)
                wait(act, unit_done, b * UNITS + u - 1)
                act.copy(xt[:, u % 2, :], bank[u % 2][:]).then_inc(xt_in, 1)

            def first_part(b, half, v):
                n = (2 * b + half) * GROUPS + v
                act.wait_ge(iw_done, n + 1)
                wait(act, brest_in, n - 1)
                act.copy(b1[:, v % 2, :], bank[6 + v % 2][0:BROWS, :]).then_inc(b1_in, 1)

            def second_part(b, half, v):
                n = (2 * b + half) * GROUPS + v
                act.wait_ge(brest_in, n + 1)
                wait(act, b_in, n - 1)
                act.copy(b2[:, v % 2, :], brest[:, v % 2, :]).then_inc(b2_in, 1)

            def inverse(b, last):
                for u in range(UNITS):
                    if u + 1 < UNITS:
                        take_x(b, u + 1)
                    elif not last:
                        take_x(b + 1, 0)
                    v = u // 2 % GROUPS
                    step = second_part if u % 2 else first_part
                    if u < UNITS // 2:
                        step(b, 1, v)
                    elif not last:
                        step(b + 1, 0, v)

            first_part(0, 0, 0)
            for v in range(GROUPS):
                if v + 1 < GROUPS:
                    first_part(0, 0, v + 1)
                second_part(0, 0, v)
            take_x(0, 0)
            inverse(0, False)
            with act.Fori(1, NB - 1) as b:
                inverse(b, False)
            inverse(NB - 1, True)

        @block.vector
        def _(dve):
            def exact_copy(dst, src):
                return dve.tensor_scalar(dst, src, 1.0, None, ALU.mult)

            def negative(dst, src):
                return dve.tensor_scalar(dst, src, -1.0, None, ALU.mult)

            def forward(b):
                for j in range(0, 8, 2):
                    dve.wait_ge(turn_done, 8 * b + j + 1)
                    put_turned(dve.tensor_copy, j).then_inc(turn_dve, 1)
                dve.wait_ge(w_done, b + 1)

            with dve.Fori(0, NB) as b:
                forward(b)

            def kernels(q, buf):
                wait(dve, mix_done, q - 1)
                dve.wait_ge(kt_group, 3 * q + 2)
                put_kernels(dve.tensor_copy, 1, buf).then_inc(kt_dve, 1)

            def stationaries(q, s, k):
                wait(dve, mix_done, q[0] - 1)
                stationary(negative, q, s, k, 1, 1, 0).then_inc(mstat_dve, 1)

            def take_mixed(q, buf):
                dve.wait_ge(mix_done, q + 1)
                wait(dve, y_turned, q - 1)
                dve.tensor_copy(mixed[buf][:, 0:KH * C], bank[MIX_BANKS[buf]][:, 0:KH * C]).then_inc(mixed_in, 1)

            def outputs(buf, row=None):
                base = buf if row is None else buf[:, row * YW:(row + 1) * YW]
                by = base.rearrange("p (x r b) -> p x r b", r=2, b=NB)
                return by[:, :, 0], by[:, :, 1]

            def combine(k):
                wait(dve, y1_in, k)
                wait(dve, yrest_in, k)
                cos_row = ysum[:, 0:YW]
                with_cos, with_sin = outputs(ysum, 1)
                (plus_re, plus_im), (minus_re, minus_im) = outputs(yplus), outputs(yminus)
                if isinstance(k, int) and k == 0:
                    dve.wait_ge(y_in, 1)
                    dve.tensor_copy(cos_row, yplus).then_inc(ysum_in, 1)
                elif isinstance(k, int) and k == 10:
                    dve.wait_ge(y_in, 20)
                    dve.tensor_copy(cos_row, yminus)
                    dve.tensor_scalar(with_sin, minus_re, -1.0, None, ALU.mult)
                    dve.tensor_copy(with_cos, minus_im).then_inc(ysum_in, 1)
                else:
                    dve.wait_ge(y_in, 2 * k + 1)
                    dve.tensor_tensor(cos_row, yplus, yminus, ALU.add)
                    dve.tensor_tensor(with_sin, plus_re, minus_re, ALU.subtract)
                    dve.tensor_tensor(with_cos, minus_im, plus_im, ALU.subtract).then_inc(ysum_in, 1)

            def rests(k, par, rows):
                dve.wait_ge(y1_in, k + 1)
                wait(dve, y2_in, k)
                wait(dve, y3_in, k)
                for h in range(2):
                    last = dve.tensor_tensor(y_from(yrest, h, rows), y_from(ysum, h, rows),
                                             y_to(par, h, 1, rows), ALU.subtract)
                last.then_inc(yrest_in, 1)
                for h in range(2):
                    last = dve.tensor_copy(y_to(par, h, 3, rows), y_to(par, h, 1, rows))
                last.then_inc(y1_again, 1)

            def third_parts(k, par, rows):
                dve.wait_ge(y2_in, k + 1)
                for h in range(2):
                    last = dve.tensor_tensor(y_to(par, h, 0, rows), y_from(yrest, h, rows),
                                             y_to(par, h, 2, rows), ALU.subtract)
                last.then_inc(y3_in, 1)

            def take_spread(k, i):
                dve.wait_ge(s_done, (0 if isinstance(k, int) and k == 0 else 8 * k - 4) + i + 1)
                put_spread(exact_copy, i, k).then_inc(s_dve, 1)

            def step(k, par, minus_ten=False):
                first, second = isinstance(k, int) and k == 1, isinstance(k, int) and k == 2
                rows = 1 if first else 2
                take_mixed(2 * k - 2, 0)
                kernels(2 * k, 0)
                combine(k - 1)
                if not first:
                    take_spread(0 if second else k - 2, 1)
                    take_spread(0 if second else k - 2, 3)
                stationaries((2 * k, 0), 1, k)
                take_mixed(2 * k - 1, 1)
                rests(k - 1, 1 - par, rows)
                kernels(2 * k + 1, 1)
                if not (first or second):
                    take_spread(k - 2, 5)
                stationaries((2 * k + 1, 1), int(minus_ten), k + 1)
                third_parts(k - 1, 1 - par, rows)
                if not (first or second):
                    take_spread(k - 2, 7)

            dve.wait_ge(h_done, NB * (TILES // 2))
            dve.wait_ge(modes_in, NB)
            stationaries((0, 0), 0, 0)
            stationaries((1, 1), 0, 1)
            kernels(0, 0)
            kernels(1, 1)
            dve.wait_ge(zeroed, 4)
            step(1, 1)
            step(2, 0)
            with dve.Fori(0, 3) as i:
                step(2 * i + 3, 1)
                step(2 * i + 4, 0)
            step(9, 1, minus_ten=True)
            take_mixed(18, 0)
            take_mixed(19, 1)
            combine(9)
            take_spread(8, 1)
            take_spread(8, 3)
            rests(9, 1, 2)
            take_spread(8, 5)
            take_spread(8, 7)
            combine(10)
            third_parts(9, 1, 2)
            rests(10, 0, 2)
            for i in (1, 3, 5, 7):
                take_spread(9, i)
            third_parts(10, 0, 2)
            for i in (1, 3, 5, 7):
                take_spread(10, i)

            def copy_six(b, half, v):
                n = (2 * b + half) * GROUPS + v
                wait(dve, iw_done, n - 1)
                src = sub(spec[0:SROWS, :], b * SB + 8 * v * ROWS, [[ROWS, 8], [0, 6], [1, ROWS]])
                exact_copy(copies[:, v % 2, :].rearrange("p (a r k) -> p a r k", r=6, k=ROWS),
                           src).then_inc(copies_in, 1)

            def rest(b, half, v):
                n = (2 * b + half) * GROUPS + v
                dve.wait_ge(b1_in, n + 1)
                wait(dve, b_in, n - 1)
                dve.scalar_tensor_tensor(brest[:, v % 2, :], b1[:, v % 2, :], part[:, 0:1],
                                         bank[6 + v % 2][0:BROWS, :], ALU.mult, ALU.add).then_inc(brest_in, 1)

            def row_part(b, half, v):
                n = (2 * b + half) * GROUPS + v
                dve.wait_ge(b2_in, n + 1)
                dve.scalar_tensor_tensor(sub(bst[half], 4 * v, [[1, 4], [C, P]]),
                                         b2[:, v % 2, :].rearrange("p (c w) -> p c w", c=4), part[:, 1:2],
                                         brest[:, v % 2, :].rearrange("p (c w) -> p c w", c=4),
                                         ALU.mult, ALU.add).then_inc(b_in, 1)

            def add_x(b, u):
                j = u // 4
                at = j % SLOTS * TILE + (u % 4) * UNIT
                dve.wait_ge(unit_done, b * UNITS + u + 1)
                dve.tensor_tensor(ring[:, at:at + UNIT], bank[2 + u % 4][:], ring[:, at:at + UNIT],
                                  ALU.add).then_inc(added, 1)

            def inverse(b, last):
                for u in range(UNITS):
                    v = u // 2 % GROUPS
                    step = row_part if u % 2 else rest
                    if u < UNITS // 2:
                        step(b, 1, v)
                    elif not last:
                        step(b + 1, 0, v)
                    if u % 2 == 0:
                        ahead = u // 2 + 2 + GROUPS
                        if ahead < 2 * GROUPS:
                            copy_six(b, 1, ahead % GROUPS)
                        elif not last:
                            copy_six(b + 1, ahead // GROUPS - 2, ahead % GROUPS)
                    add_x(b, u)

            dve.wait_ge(s_act, 4 * 10 + 2)
            dve.wait_ge(s_dve, 4 * 10 + 2)
            copy_six(0, 0, 0)
            copy_six(0, 0, 1)
            rest(0, 0, 0)
            for v in range(GROUPS):
                if v + 2 < GROUPS:
                    copy_six(0, 0, v + 2)
                if v + 1 < GROUPS:
                    rest(0, 0, v + 1)
                row_part(0, 0, v)
            copy_six(0, 1, 0)
            copy_six(0, 1, 1)
            inverse(0, False)
            with dve.Fori(1, NB - 1) as b:
                inverse(b, False)
            inverse(NB - 1, True)


def tables():
    import numpy as np

    def parts(a):
        a = a.astype(np.float32)
        p = []
        for _ in range(3):
            p.append(((a.view(np.uint32) + 0x8000) & 0xFFFF0000).view(np.float32))
            a = a - p[-1]
        return p

    def angle(f, n):
        return 2 * np.pi * (np.outer(f, n) % 256) / 256

    n = np.arange(256)
    k, kx = np.arange(KP), np.arange(KX)
    row_h = np.concatenate([np.cos(angle(k, n)), np.sin(angle(k[1:], n))])
    t_h = np.zeros((P, 2, 32), np.float32)
    t_h[:, :, 0:ROWS] = row_h.reshape(ROWS, 2, P).transpose(2, 1, 0)
    c, s = np.cos(angle(kx, n)), np.sin(angle(kx, n))
    v = np.stack([np.stack([c, c]), np.stack([-s, -s]), np.stack([-s, s]), np.stack([-c, c])])
    t_w = v.reshape(4, 2 * KX, 2, P).transpose(3, 2, 0, 1).astype(np.float32)
    weight = np.where(kx == 0, 1.0, 2.0)[:, None] / (H * W)
    order = [4 * kh + g for odd in range(2) for kh in range(odd, KH, 2) for g in range(4)]
    g = parts(np.stack([weight * c, -weight * s], 1)[order].reshape(2 * KX, W))
    t_iw = np.stack([np.concatenate([g[0], g[0], g[0]]), np.concatenate([g[1], g[1], g[2]])], 1)
    f = parts(row_h)
    t_ih = np.concatenate([f[0], f[0], f[0], f[1], f[1], f[2]]).reshape(BROWS, 2, P)
    p = np.array([[0, 0], [-1, 0], [-1, -1], [0, 0], [-1, 0], [0, 0]], np.float32)
    t_part = np.repeat(p, ROWS, axis=0)
    t_sel = np.concatenate([np.eye(C), np.eye(C)]).astype(np.float32)
    return dict(t_h=t_h, t_w=t_w, t_id=np.eye(P, dtype=np.float32), t_sel=t_sel, t_iw=t_iw, t_ih=t_ih, t_part=t_part)


def kernel(x, L0_conv_kernel_real, L0_conv_kernel_imag, L0_conv_w_lin):
    import numpy as np
    import concourse.bacc as bacc
    from concourse.bass_utils import run_bass_kernel_spmd

    nc = bacc.Bacc("TRN2", target_bir_lowering=False, num_devices=1)
    given = dict(x=x, k_re=L0_conv_kernel_real, k_im=L0_conv_kernel_imag, w_lin=L0_conv_w_lin)
    arrays, args = {}, {}
    for name, a in {**given, **tables()}.items():
        a = np.ascontiguousarray(a)
        arrays[f"in_{name}"] = a
        args[name] = nc.dram_tensor(f"in_{name}", a.shape, mybir.dt.from_np(a.dtype), kind="ExternalInput").ap()
    args["out"] = nc.dram_tensor("out_y", args["x"].shape, F32, kind="ExternalOutput").ap()
    spectral_conv(nc, **args)
    r = run_bass_kernel_spmd(nc, [arrays], core_ids=[0])
    return r.results[0]["out_y"]
```

```python
from contextlib import ExitStack

import concourse.bass as bass
from concourse import mybir

F32 = mybir.dt.float32
BF16 = mybir.dt.bfloat16
ALU = mybir.AluOpType

P = 128
H = W = 256
C = 64
KX = 20
KP = 11
ROWS = 2 * KP - 1
TILE_W = 32
TILE = TILE_W * C
SLOTS = 8
TILES = 2 * W // TILE_W
UNIT = 512
UNITS = TILES * TILE // UNIT
SLOTS_3 = 4
GC = 2
GROUPS = C // GC
BROWS = 6 * ROWS
PKX = KX // 2 * 2
SECOND = 64
SROWS = SECOND + 3 * PKX
KH = KX // 4
PAIRS = (KH + 1) // 2
YCOLS = 2 * 4 * PKX


def wait(eng, sem, value):
    if not (isinstance(value, int) and value <= 0):
        eng.wait_ge(sem, value)


def sub(base, offset, dims):
    return bass.AP(base.tensor, base.offset + offset, [list(base.ap[0])] + dims)


def spectral_conv(nc, x, k_re, k_im, w_lin, t_h, t_w, t_id, t_sel, t_iw, t_ih, t_part, out):
    NB = x.shape[0]
    BH = NB // 2
    RB = NB * YCOLS
    SB = 2 * C * ROWS
    with ExitStack() as ctx:
        def sb(name, shape, dt):
            return ctx.enter_context(nc.sbuf_tensor(name, shape, dt))

        def sem(name):
            return ctx.enter_context(nc.semaphore(name))

        bank = [ctx.enter_context(nc.psum_tensor(f"bank{i}", [P, UNIT], F32)) for i in range(8)]

        dft_h = sb("dft_h", [P, 2, 32], F32)
        dft_w = sb("dft_w", [P, 2, 4, 2 * KX], F32)
        ident = sb("ident", [P, P], F32)
        sel = sb("sel", [P, C], BF16)
        inv_w = sb("inv_w", [SROWS, 2, W], BF16)
        inv_h = sb("inv_h", [BROWS, 2, P], BF16)
        part = sb("part", [BROWS, 2], F32)
        w_nat = sb("w_nat", [P, P], F32)
        w_blk = sb("w_blk", [P, P], F32)

        ring = sb("ring", [P, SLOTS * TILE], F32)
        KN = KX * C * C // P
        offset = 0

        def stage_two(words):
            nonlocal offset
            offset += words
            assert offset <= SLOTS * TILE
            return ring[:, offset - words:offset]

        YW = PAIRS * P
        kbuf = [stage_two(2 * KN) for _ in range(2)]
        lbuf = [stage_two(KX * C) for _ in range(2)]
        mstat = [stage_two(KX * 2 * NB) for _ in range(2)]
        mixed = [stage_two(YW) for _ in range(2)]
        ypart = [stage_two(RB).bitcast(BF16) for _ in range(2)]
        yplus = stage_two(YW)
        yminus = stage_two(YW)
        ysum = stage_two(2 * YW)

        even_image = sb("even_image", [P, W * C], BF16)
        bst = [even_image[0:BROWS, :], ring[0:BROWS, SLOTS_3 * TILE:SLOTS_3 * TILE + W * C // 2].bitcast(BF16)]
        modes = even_image[:, 0:2 * 2 * KP * KX * NB].bitcast(F32)

        spec = sb("spec", [P, max(16, NB) * SB], BF16)
        hrow = spec[:, 0:2 * 16 * W].bitcast(F32)
        hcol = spec[:, 2 * 16 * W:2 * 16 * W + 4 * ROWS * C].bitcast(F32)

        xt = sb("xt", [P, 2, UNIT], F32)
        yrest = xt[:].rearrange("p a b -> p (a b)")[:, 0:2 * YW]
        copies = sb("copies", [SROWS, 2, 2 * GC * BROWS], BF16)
        eo = sb("eo", [BROWS, 2, UNIT], F32)
        brest = sb("brest", [BROWS, 2, UNIT], F32)
        b1 = sb("b1", [BROWS, 2, UNIT], BF16)
        b2 = sb("b2", [BROWS, 2, UNIT], BF16)

        dft_h_in = sem("dft_h_in")
        tables_in = sem("tables_in")
        cast_in = sem("cast_in")
        w_zeroed = sem("w_zeroed")
        w_turned = sem("w_turned")
        w_ready = sem("w_ready")
        x_in = [sem(f"x_in{s}") for s in range(SLOTS)]
        h_done = sem("h_done")
        h_evac = sem("h_evac")
        turn_done = sem("turn_done")
        turn_act = sem("turn_act")
        turn_dve = sem("turn_dve")
        w_done = sem("w_done")
        modes_in = sem("modes_in")
        k_in = [sem(f"k_in{q}") for q in range(2)]
        kt_group = sem("kt_group")
        kt_act = sem("kt_act")
        kt_dve = sem("kt_dve")
        mstat_act = sem("mstat_act")
        mstat_dve = sem("mstat_dve")
        mix_done = sem("mix_done")
        mixed_in = sem("mixed_in")
        y_turned = sem("y_turned")
        y_in = sem("y_in")
        ysum_in = sem("ysum_in")
        y1_in = sem("y1_in")
        y1_again = sem("y1_again")
        yrest_in = sem("yrest_in")
        y2_in = sem("y2_in")
        y3_in = sem("y3_in")
        zeroed = sem("zeroed")
        s_done = sem("s_done")
        s_act = sem("s_act")
        s_dve = sem("s_dve")
        xt_done = sem("xt_done")
        xt_in = sem("xt_in")
        unit_done = sem("unit_done")
        added = sem("added")
        stored = [sem(f"stored{s}") for s in range(SLOTS_3)]
        copies_in = sem("copies_in")
        iw_done = sem("iw_done")
        eo_in = sem("eo_in")
        full_in = sem("full_in")
        b1_in = sem("b1_in")
        brest_in = sem("brest_in")
        b2_in = sem("b2_in")
        b_in = sem("b_in")

        def slot(s):
            return ring[:, s * TILE:(s + 1) * TILE]

        def x_tile(t, b, j):
            hh, wq = j % 2, j // 2
            return t[bass.ds(b, 1), hh * P:(hh + 1) * P, wq * TILE_W:(wq + 1) * TILE_W, :].rearrange(
                "b h w c -> h (b w c)")

        def put_turned(copy, j):
            wh = j // 4
            src = bank[2 + j % 4][:].rearrange("p (q g m) -> p q g m", q=4, g=4)[:, :, :, 0:ROWS]
            return copy(sub(hcol, wh * ROWS * C + 4 * (j % 4), [[1, 4], [16, 4], [C, ROWS]]), src)

        K_BANKS, MIX_BANK, Y_BANK, S_BANKS = (0, 1, 0), 2, 3, (6, 7, 4, 5)
        CHUNKS = 4 + 8 * 10

        def first_chunk(c):
            return 0 if isinstance(c, int) and c == 0 else 8 * c - 4

        def put_kernels(copy, j, buf):
            n = min(UNIT, KX * C - UNIT * j)
            return copy(lbuf[buf][:, UNIT * j:UNIT * j + n], bank[K_BANKS[j]][:, 0:n])

        def put_spread(copy, c, i):
            row, odd, bh = i // 4, i // 2 % 2, i % 2
            ky = (0, 10)[c] if isinstance(c, int) and c < 2 else c - 1
            kyr = ky + 10 * row
            src = bank[S_BANKS[i % 4]][0:SROWS, 0:BH * C].rearrange("p (b c) -> p b c", c=C)
            return copy(sub(spec[0:SROWS, :], kyr + bh * BH * SB + odd * ROWS, [[SB, BH], [2 * ROWS, C]]), src)

        def group(stage, b, m):
            if not (isinstance(b, int) and b + m // GROUPS >= NB):
                stage(b + m // GROUPS, GROUPS * b + m, m % GROUPS)

        def stationary(copy, q, s, k, ri, half, ro):
            buf = q[1]
            src = modes[ri * C:(ri + 1) * C, bass.ds((s * KP + k) * KX * NB, KX * NB)]
            dst = mstat[buf].rearrange("p (x r b) -> p x r b", r=2, b=NB)[half * C:(half + 1) * C, :, ro]
            return copy(dst, src.rearrange("p (x b) -> p x b", b=NB))

        def y_dims(h, rows, step, odd_step):
            return [[step, rows * NB], [odd_step, 2], [1, 4 * (PAIRS if h == 0 else KH // 2)]]

        def y_to(par, h, rep, rows):
            return sub(ypart[par][h * C:(h + 1) * C, :], rep * PKX + h * 4 * PAIRS,
                       y_dims(h, rows, YCOLS, 4 * PKX))

        def y_from(buf, h, rows):
            return sub(buf[h * C:(h + 1) * C, :], 0, y_dims(h, rows, YW // NB, 4 * PAIRS))

        block = ctx.enter_context(nc.Block())

        @block.sync
        def _(sp):
            def load(b, j, slots=SLOTS):
                sp.dma_start(slot(j % slots), x_tile(x, b, j)).then_inc(x_in[j % slots], 16)

            sp.dma_start(dft_h[:], t_h).then_inc(dft_h_in, 16)
            for j in range(SLOTS):
                load(0, j)
            for dst, src in ((ident, t_id), (dft_w, t_w), (part, t_part)):
                sp.dma_start(dst[:], src).then_inc(tables_in, 16)
            sp.wait_ge(w_zeroed, 1)
            for e in range(2):
                sp.dma_start(w_nat[e * C:(e + 1) * C, e * C:(e + 1) * C], w_lin).then_inc(tables_in, 16)

            def forward(b, last):
                for t in range(TILES // 2):
                    later = t + SLOTS // 2
                    if last and later >= TILES // 2:
                        break
                    sp.wait_ge(h_done, b * (TILES // 2) + t + 1)
                    for hh in range(2):
                        if later < TILES // 2:
                            load(b, 2 * later + hh)
                        else:
                            load(b + 1, 2 * (later - TILES // 2) + hh)

            with sp.Fori(0, NB - 1) as b:
                forward(b, False)
            forward(NB - 1, True)

            def kernels(q, row):
                for t, src in enumerate((k_re, k_im)):
                    flat = src[bass.ds(row, 1)].rearrange("x y i j -> (x y i) j").rearrange("(s p) j -> p s j", p=P)
                    dst = kbuf[q].rearrange("p (s t j) -> p s t j", t=2, j=C)[:, :, t, :]
                    sp.dma_start(dst, flat).then_inc(k_in[q], 16)

            assert 2 * 2 * KN <= 2 * TILE
            sp.wait_ge(h_done, NB * (TILES // 2) - 3)
            kernels(0, 10)
            kernels(1, 0)
            with sp.Fori(1, 10) as k:
                minus_k = sp.snap(k * -1 + 10)
                sp.wait_ge(kt_group, 6 * k - 3)
                kernels(0, 10 + k)
                sp.wait_ge(kt_group, 6 * k)
                kernels(1, minus_k)

            sp.wait_ge(s_done, CHUNKS)
            for j in range(SLOTS_3):
                load(0, j, SLOTS_3)

            def inverse(b, first, last):
                for j in range(TILES):
                    sp.wait_ge(added, b * UNITS + 4 * (j + 1))
                    sp.dma_start(x_tile(out, b, j), slot(j % SLOTS_3)).then_inc(stored[j % SLOTS_3], 16)
                    if (first and j == 0) or (last and j + SLOTS_3 - 1 >= TILES):
                        continue
                    before = (j - 1) % SLOTS_3
                    n = TILES // SLOTS_3 * b + (j - 1) // SLOTS_3 + 1
                    sp.wait_ge(stored[before], 16 * n)
                    j2 = j + SLOTS_3 - 1
                    load(b if j2 < TILES else b + 1, j2 % TILES, SLOTS_3)

            inverse(0, True, False)
            with sp.Fori(1, NB - 1) as b:
                inverse(b, False, False)
            inverse(NB - 1, False, True)
            for s in range(SLOTS_3):
                sp.wait_ge(stored[s], 16 * TILES // SLOTS_3 * NB)

        @block.gpsimd
        def _(pool):
            pool.memset(w_nat[:], 0.0).then_inc(w_zeroed, 1)
            for dst, src in ((sel, t_sel), (inv_w, t_iw), (inv_h, t_ih)):
                pool.dma_start(dst[:], src).then_inc(cast_in, 16)
            pool.wait_ge(h_done, NB * (TILES // 2))
            for q in range(2):
                pool.memset(mixed[q][:, KH * C:], 0.0).then_inc(zeroed, 1)

            for par in range(2):
                pool.memset(ypart[par], 0.0).then_inc(zeroed, 1)

            def add_and_subtract(b, n, v):
                pool.wait_ge(eo_in, n - GROUPS + 1)
                wait(pool, b_in, n - 1)
                even, odd = (eo[:, v % 2, i * GC * P:(i + 1) * GC * P].rearrange("p (c w) -> p c w", c=GC)
                             for i in range(2))
                to = brest[:, v % 2, :].rearrange("p (c s w) -> p c s w", s=2, w=P)
                pool.tensor_tensor(to[:, :, 0], even, odd, ALU.add).then_inc(full_in, 1)
                pool.tensor_tensor(to[:, :, 1], even, odd, ALU.subtract).then_inc(full_in, 1)

            def inverse(b):
                for m in range(GROUPS):
                    group(add_and_subtract, b, m + GROUPS + 2)

            for n in range(GROUPS, GROUPS + 2):
                group(add_and_subtract, 0, n)
            inverse(0)
            with pool.Fori(1, NB - 3) as b:
                inverse(b)
            for b in range(NB - 3, NB):
                inverse(b)

        @block.tensor
        def _(pe):
            pe.wait_ge(dft_h_in, 16)

            def turn_kernels(q, kin, first=False):
                q, buf = q
                pe.wait_ge(k_in[buf], 32 * kin)
                for j in range(3):
                    if j == 2:
                        pe.wait_ge(kt_act, 2 * q + 1)
                    elif not first:
                        pe.wait_ge(*((kt_act, 2 * q), (kt_dve, q))[j])
                    for s in range(4 * j, min(4 * j + 4, KX // 2)):
                        last = pe.transpose(bank[K_BANKS[j]][:, P * (s - 4 * j):P * (s - 4 * j + 1)],
                                            kbuf[buf][:, s * P:(s + 1) * P], ident[:])
                    last.then_inc(kt_group, 1)

            def h_transform(b, pairs):
                for t in pairs:
                    for hh in range(2):
                        s = 2 * (t % (SLOTS // 2)) + hh
                        pe.wait_ge(x_in[s], 16 * (2 * b + t // (SLOTS // 2) + 1))
                    if t > 1:
                        pe.wait_ge(h_evac, b * (TILES // 2) + t - 1)
                    for hh in range(2):
                        tile = slot(2 * (t % (SLOTS // 2)) + hh).rearrange("p (w c) -> p w c", c=C)
                        for g in range(4):
                            last = pe.matmul(bank[t % 2][32 * g:32 * g + 32, :], dft_h[:, hh, :],
                                             tile[:, :, 16 * g:16 * g + 16], start=hh == 0, stop=hh == 1,
                                             tile_position=(0, 32 * g))
                    last.then_inc(h_done, 1)

            def forward(b, final=False):
                h_transform(b, range(2, TILES // 2))
                pe.wait_ge(h_evac, (b + 1) * (TILES // 2))
                pe.wait_ge(tables_in, 5 * 16)
                for j in range(8):
                    if j >= 4:
                        pe.wait_ge(turn_act if j % 2 else turn_dve, 4 * b + (j - 4) // 2 + 1)
                    wh = j // 4
                    for q in range(4):
                        c16 = 4 * (j % 4) + q
                        last = pe.transpose(bank[2 + j % 4][:, P * q:P * (q + 1)],
                                            hrow[:, c16 * W + wh * P:c16 * W + (wh + 1) * P], ident[:])
                    last.then_inc(turn_done, 1)
                if final:
                    turn_kernels((0, 0), 1, first=True)
                    turn_kernels((1, 1), 1)
                else:
                    h_transform(b + 1, range(2))
                pe.wait_ge(turn_act, 4 * (b + 1))
                pe.wait_ge(turn_dve, 4 * (b + 1))
                for k in range(KP):
                    rows = [(0, k)] + [(1, KP - 1 + k)] * (k > 0)
                    todo = [(wh, sc, m) for wh in range(2) for sc, m in rows]
                    for n, (wh, sc, m) in enumerate(todo):
                        for ri in range(2):
                            last = pe.matmul(bank[6][ri * C:(ri + 1) * C, 2 * KX * k:2 * KX * (k + 1)],
                                             hcol[:, (wh * ROWS + m) * C:(wh * ROWS + m + 1) * C],
                                             dft_w[:, wh, 2 * sc + ri, :],
                                             start=n == 0, stop=n == len(todo) - 1, tile_position=(0, ri * C))
                last.then_inc(w_done, 1)
                pe.wait_ge(modes_in, b + 1)

            h_transform(0, range(2))
            with pe.Fori(0, NB - 1) as b:
                forward(b)
            forward(NB - 1, final=True)

            pe.transpose(bank[7][:, 0:P], w_nat[:], ident[:]).then_inc(w_turned, 1)

            def mix(q):
                q, buf = q
                pe.wait_ge(kt_act, 2 * q + 2)
                pe.wait_ge(kt_dve, q + 1)
                pe.wait_ge(mstat_act, q + 1)
                pe.wait_ge(mstat_dve, q + 1)
                wait(pe, mixed_in, q)
                for i in range(KX):
                    g, kh = i % 4, i // 4
                    kx = 4 * kh + 2 * (g % 2) + g // 2
                    last = pe.matmul(bank[MIX_BANK][32 * g:32 * g + 2 * NB, kh * C:(kh + 1) * C],
                                     mstat[buf][:, kx * 2 * NB:(kx + 1) * 2 * NB],
                                     lbuf[buf][:, kx * C:(kx + 1) * C],
                                     start=True, stop=True, tile_position=(0, 32 * g))
                last.then_inc(mix_done, 1)

            def turn_mixed(q):
                q, buf = q
                pe.wait_ge(mixed_in, q + 1)
                wait(pe, y_in, q)
                for pair in range(PAIRS):
                    last = pe.transpose(bank[Y_BANK][:, pair * P:(pair + 1) * P],
                                        mixed[buf][:, pair * P:(pair + 1) * P], ident[:])
                last.then_inc(y_turned, 1)

            def spread(c, par, row):
                if row == 0:
                    pe.wait_ge(y3_in, 2 * c + 2)
                    pe.wait_ge(y1_again, c + 1)
                for i in range(4 * row, 4 * row + 4):
                    odd, bh = i // 2 % 2, i % 2
                    wait(pe, s_dve if bh else s_act,
                         (0 if isinstance(c, int) and c == 0 else 4 * c - 2) + i // 2 - 1)
                    for b in range(BH):
                        o = row * RB + (bh * BH + b) * YCOLS + odd * 4 * PKX
                        for at, skip, n in ((0, 0, SECOND), (SECOND, PKX, 3 * PKX)):
                            last = pe.matmul(bank[S_BANKS[i % 4]][at:at + n, b * C:(b + 1) * C],
                                             ypart[par][:, o + skip:o + skip + n], sel[:],
                                             start=True, stop=True, tile_position=(0, at))
                    last.then_inc(s_done, 1)

            def step(k, par):
                c = k - 1
                only_cos = isinstance(k, int) and k == 1
                turn_kernels((2 * k + 1, 1), k + 1)
                turn_mixed((2 * k - 1, 1))
                spread(c, 1 - par, 0)
                mix((2 * k, 0))
                if not (isinstance(k, int) and k == 9):
                    turn_kernels((2 * k + 2, 0), k + 2)
                turn_mixed((2 * k, 0))
                if not only_cos:
                    spread(c, 1 - par, 1)
                mix((2 * k + 1, 1))

            mix((0, 0))
            turn_kernels((2, 0), 2)
            pe.wait_ge(zeroed, 4)
            turn_mixed((0, 0))
            mix((1, 1))
            pe.wait_ge(w_ready, 1)
            pe.wait_ge(cast_in, 3 * 16)
            step(1, 1)
            step(2, 0)
            with pe.Fori(0, 3) as i:
                step(2 * i + 3, 1)
                step(2 * i + 4, 0)
            step(9, 1)
            turn_mixed((19, 1))
            for c in (9, 10):
                spread(c, c % 2, 0)
                spread(c, c % 2, 1)

            def turn_x(b, u):
                if u % 4 == 0:
                    j = u // 4
                    before = 2 * NB + (TILES // SLOTS_3) * b + j // SLOTS_3
                    pe.wait_ge(x_in[j % SLOTS_3], 16 * (before + 1))
                wait(pe, xt_in, b * UNITS + u - 1)
                base = (u // 4) % SLOTS_3 * TILE + (u % 4) * UNIT
                for q in range(4):
                    last = pe.transpose(bank[u % 2][:, P * q:P * (q + 1)],
                                        ring[:, base + P * q:base + P * (q + 1)], ident[:])
                last.then_inc(xt_done, 1)

            def inverse_w(b, n, v):
                if isinstance(n, int) and n < GROUPS + 2:
                    pe.wait_ge(brest_in, n - 1)
                else:
                    pe.wait_ge(eo_in, n - GROUPS - 1)
                pe.wait_ge(copies_in, n + 1)
                for c in range(GC):
                    for odd in range(2):
                        at = (2 * c + odd) * BROWS
                        o = (GC * odd + c) * P
                        last = pe.matmul(bank[6 + v % 2][0:BROWS, o:o + P], copies[:, v % 2, at:at + BROWS],
                                         inv_w[:, odd, 0:P], start=True, stop=True)
                last.then_inc(iw_done, 1)

            def first_inverse_w(n):
                wait(pe, brest_in, n - 1)
                pe.wait_ge(copies_in, n + 1)
                for c in range(GC):
                    for odd in range(2):
                        at = (2 * c + odd) * BROWS
                        last = pe.matmul(bank[6 + n % 2][0:BROWS, c * W:(c + 1) * W],
                                         copies[:, n % 2, at:at + BROWS], inv_w[:, odd, :],
                                         start=odd == 0, stop=odd == 1)
                last.then_inc(iw_done, 1)

            def sum_unit(b, par, u):
                j = u // 4
                hh, wq = j % 2, j // 2
                if u == 0:
                    pe.wait_ge(b_in, (b + 1) * GROUPS)
                wait(pe, added, b * UNITS + u - 3)
                at = (wq * TILE_W * C) + (u % 4) * UNIT
                o = bank[2 + u % 4]
                pe.matmul(o[:], inv_h[:, hh, :], bst[par][:, at:at + UNIT], start=True, stop=False)
                pe.wait_ge(xt_in, b * UNITS + u + 1)
                for q in range(4):
                    last = pe.matmul(o[:, P * q:P * (q + 1)], xt[:, u % 2, P * q:P * (q + 1)], w_blk[:],
                                     start=False, stop=q == 3)
                last.then_inc(unit_done, 1)

            def inverse(b, par, last=False):
                for u in range(UNITS):
                    if u + 1 < UNITS:
                        turn_x(b, u + 1)
                    elif not last:
                        turn_x(b + 1, 0)
                    if u % 2 == 0:
                        group(inverse_w, b, u // 2 + GROUPS + 2)
                    sum_unit(b, par, u)

            for n in range(GROUPS):
                first_inverse_w(n)
            for n in range(GROUPS, GROUPS + 2):
                group(inverse_w, 0, n)
            turn_x(0, 0)
            inverse(0, 0)
            with pe.Fori(0, (NB - 4) // 2) as i:
                inverse(2 * i + 1, 1)
                inverse(2 * i + 2, 0)
            for b in range(NB - 3, NB):
                inverse(b, b % 2, last=b == NB - 1)

        @block.scalar
        def _(act):
            def kernels(q, buf):
                wait(act, mix_done, q - 1)
                for j in (0, 2):
                    act.wait_ge(kt_group, 3 * q + j + 1)
                    put_kernels(act.copy, j, buf).then_inc(kt_act, 1)

            def take_h(b, pairs):
                for t in pairs:
                    act.wait_ge(h_done, b * (TILES // 2) + t + 1)
                    act.copy(sub(hrow, t * TILE_W, [[1, TILE_W], [W, 16]]),
                             bank[t % 2][:].rearrange("p (w c) -> p w c", c=16)).then_inc(h_evac, 1)

            def forward(b, final=False):
                take_h(b, range(2, TILES // 2))
                for j in range(1, 8, 2):
                    act.wait_ge(turn_done, 8 * b + j + 1)
                    put_turned(act.copy, j).then_inc(turn_act, 1)
                if final:
                    kernels(0, 0)
                    kernels(1, 1)
                else:
                    take_h(b + 1, range(2))
                act.wait_ge(w_done, b + 1)
                src = bank[6][:, 0:KP * 2 * KX].rearrange("p (k s x) -> p k s x", s=2, x=KX)
                dst = modes.rearrange("p (s k x b) -> p k s x b", s=2, k=KP, b=NB)[:, :, :, :, bass.ds(b, 1)]
                for s in range(2):
                    last = act.copy(dst[:, :, s].rearrange("p k x b -> p k (x b)"), src[:, :, s])
                last.then_inc(modes_in, 1)

            take_h(0, range(2))
            with act.Fori(0, NB - 1) as b:
                forward(b)
            forward(NB - 1, final=True)

            def stationaries(q, s, k):
                wait(act, mix_done, q[0] - 1)
                stationary(act.copy, q, s, k, 0, 0, 0)
                stationary(act.copy, q, s, k, 1, 0, 1)
                stationary(act.copy, q, s, k, 0, 1, 1).then_inc(mstat_act, 1)

            def take_turned(q, dst, used):
                act.wait_ge(y_turned, q + 1)
                wait(act, ysum_in, used)
                src = bank[Y_BANK][:, 0:YW].rearrange("p (x o n b) -> p x o n b", o=2, n=4, b=NB)
                for odd in range(2):
                    last = act.copy(sub(dst, odd * 4 * PAIRS, [[4, PAIRS], [1, 4], [YW // NB, NB]]), src[:, :, odd])
                last.then_inc(y_in, 1)

            def first_parts(c, par, h, rows):
                if h == 0:
                    act.wait_ge(ysum_in, c + 1)
                    wait(act, s_done, 8 * c - 12)
                act.copy(y_to(par, h, 1, rows), y_from(ysum, h, rows)).then_inc(y1_in, 1)

            def second_parts(c, par, h, rows):
                act.wait_ge(yrest_in, 2 * c + h + 1)
                act.copy(y_to(par, h, 2, rows), y_from(yrest, h, rows)).then_inc(y2_in, 1)

            def take_spread(c, i):
                act.wait_ge(s_done, first_chunk(c) + i + 1)
                put_spread(act.copy, c, i).then_inc(s_act, 1)

            def step(k, par):
                only_cos = isinstance(k, int) and k == 1
                last = isinstance(k, int) and k == 9
                kernels(2 * k + 1, 1)
                take_turned(2 * k - 1, yminus, k)
                take_spread(k - 1, 0)
                first_parts(k, par, 0, 2)
                take_spread(k - 1, 2)
                first_parts(k, par, 1, 2)
                stationaries((2 * k + 1, 1), 1, k)
                if not last:
                    kernels(2 * k + 2, 0)
                take_turned(2 * k, yplus, k + 1)
                second_parts(k, par, 0, 2)
                if not only_cos:
                    take_spread(k - 1, 4)
                second_parts(k, par, 1, 2)
                if not last:
                    stationaries((2 * k + 2, 0), 0, k + 1)
                if not only_cos:
                    take_spread(k - 1, 6)

            act.wait_ge(w_turned, 1)
            act.copy(w_blk[:], bank[7][:, 0:P]).then_inc(w_ready, 1)
            act.wait_ge(h_done, NB * (TILES // 2))
            act.wait_ge(modes_in, NB)
            stationaries((0, 0), 0, 0)
            stationaries((1, 1), 1, 10)
            kernels(2, 0)
            stationaries((2, 0), 0, 1)
            act.wait_ge(zeroed, 4)
            take_turned(0, yplus, 0)
            for h in range(2):
                first_parts(0, 0, h, 1)
            for h in range(2):
                second_parts(0, 0, h, 1)
            step(1, 1)
            step(2, 0)
            with act.Fori(0, 3) as i:
                step(2 * i + 3, 1)
                step(2 * i + 4, 0)
            step(9, 1)
            take_turned(19, yminus, 10)
            take_spread(9, 0)
            first_parts(10, 0, 0, 2)
            first_parts(10, 0, 1, 2)
            take_spread(9, 2)
            second_parts(10, 0, 0, 2)
            second_parts(10, 0, 1, 2)
            take_spread(9, 4)
            take_spread(9, 6)
            for i in range(0, 8, 2):
                take_spread(10, i)

            def take_x(b, u):
                act.wait_ge(xt_done, b * UNITS + u + 1)
                wait(act, unit_done, b * UNITS + u - 1)
                act.copy(xt[:, u % 2, :], bank[u % 2][:]).then_inc(xt_in, 1)

            def take_eo(b, n, v):
                act.wait_ge(iw_done, n + 1)
                wait(act, full_in, 2 * (n - GROUPS) - 2)
                act.copy(eo[:, v % 2, :], bank[6 + v % 2][0:BROWS, :]).then_inc(eo_in, 1)

            def first_part(b, n, v):
                act.wait_ge(full_in, 2 * (n - GROUPS) + 2)
                wait(act, brest_in, n - 1)
                act.copy(b1[:, v % 2, :], brest[:, v % 2, :]).then_inc(b1_in, 1)

            def second_part(b, n, v):
                act.wait_ge(brest_in, n + 1)
                wait(act, b_in, n - 1)
                act.copy(b2[:, v % 2, :], brest[:, v % 2, :]).then_inc(b2_in, 1)

            def inverse(b, last):
                for u in range(UNITS):
                    if u + 1 < UNITS:
                        take_x(b, u + 1)
                    elif not last:
                        take_x(b + 1, 0)
                    m = u // 2 + GROUPS
                    if u % 2 == 0:
                        group(take_eo, b, m + 2)
                        group(first_part, b, m + 1)
                    else:
                        group(second_part, b, m + 1)

            def first_part_0(n):
                act.wait_ge(iw_done, n + 1)
                wait(act, brest_in, n - 1)
                act.copy(b1[:, n % 2, :], bank[6 + n % 2][0:BROWS, :]).then_inc(b1_in, 1)

            first_part_0(0)
            for n in range(GROUPS):
                if n + 1 < GROUPS:
                    first_part_0(n + 1)
                second_part(0, n, n)
            group(take_eo, 0, GROUPS)
            group(take_eo, 0, GROUPS + 1)
            group(first_part, 0, GROUPS)
            group(second_part, 0, GROUPS)
            take_x(0, 0)
            inverse(0, False)
            with act.Fori(1, NB - 3) as b:
                inverse(b, False)
            for b in range(NB - 3, NB):
                inverse(b, b == NB - 1)

        @block.vector
        def _(dve):
            def exact_copy(dst, src):
                return dve.tensor_scalar(dst, src, 1.0, None, ALU.mult)

            def negative(dst, src):
                return dve.tensor_scalar(dst, src, -1.0, None, ALU.mult)

            def kernels(q, buf):
                wait(dve, mix_done, q - 1)
                dve.wait_ge(kt_group, 3 * q + 2)
                put_kernels(dve.tensor_copy, 1, buf).then_inc(kt_dve, 1)

            def forward(b, final=False):
                for j in range(0, 8, 2):
                    dve.wait_ge(turn_done, 8 * b + j + 1)
                    put_turned(dve.tensor_copy, j).then_inc(turn_dve, 1)
                if final:
                    kernels(0, 0)
                    kernels(1, 1)
                dve.wait_ge(w_done, b + 1)

            with dve.Fori(0, NB - 1) as b:
                forward(b)
            forward(NB - 1, final=True)

            def stationaries(q, s, k):
                wait(dve, mix_done, q[0] - 1)
                stationary(negative, q, s, k, 1, 1, 0).then_inc(mstat_dve, 1)

            def take_mixed(q, buf):
                dve.wait_ge(mix_done, q + 1)
                wait(dve, y_turned, q - 1)
                dve.tensor_copy(mixed[buf][:, 0:KH * C], bank[MIX_BANK][:, 0:KH * C]).then_inc(mixed_in, 1)

            def outputs(buf, row=None):
                base = buf if row is None else buf[:, row * YW:(row + 1) * YW]
                by = base.rearrange("p (n r) -> p n r", r=2)
                return by[:, :, 0], by[:, :, 1]

            def combine(c):
                wait(dve, y1_in, 2 * c)
                wait(dve, yrest_in, 2 * c)
                cos_row = ysum[:, 0:YW]
                with_cos, with_sin = outputs(ysum, 1)
                (plus_re, plus_im), (minus_re, minus_im) = outputs(yplus), outputs(yminus)
                if isinstance(c, int) and c == 0:
                    dve.wait_ge(y_in, 1)
                    dve.tensor_copy(cos_row, yplus).then_inc(ysum_in, 1)
                elif isinstance(c, int) and c == 1:
                    dve.wait_ge(y_in, 2)
                    dve.tensor_copy(cos_row, yminus)
                    dve.tensor_scalar(with_sin, minus_re, -1.0, None, ALU.mult)
                    dve.tensor_copy(with_cos, minus_im).then_inc(ysum_in, 1)
                else:
                    dve.wait_ge(y_in, 2 * c)
                    dve.tensor_tensor(cos_row, yplus, yminus, ALU.add)
                    dve.tensor_tensor(with_sin, plus_re, minus_re, ALU.subtract)
                    dve.tensor_tensor(with_cos, minus_im, plus_im, ALU.subtract).then_inc(ysum_in, 1)

            def rests(c, par, rows):
                wait(dve, y2_in, 2 * c)
                wait(dve, y3_in, 2 * c)
                for h in range(2):
                    dve.wait_ge(y1_in, 2 * c + h + 1)
                    dve.tensor_tensor(y_from(yrest, h, rows), y_from(ysum, h, rows),
                                      y_to(par, h, 1, rows), ALU.subtract).then_inc(yrest_in, 1)
                for h in range(2):
                    last = dve.tensor_copy(y_to(par, h, 3, rows), y_to(par, h, 1, rows))
                last.then_inc(y1_again, 1)

            def third_parts(c, par, rows):
                for h in range(2):
                    dve.wait_ge(y2_in, 2 * c + h + 1)
                    dve.tensor_tensor(y_to(par, h, 0, rows), y_from(yrest, h, rows),
                                      y_to(par, h, 2, rows), ALU.subtract).then_inc(y3_in, 1)

            def take_spread(c, i):
                dve.wait_ge(s_done, first_chunk(c) + i + 1)
                put_spread(exact_copy, c, i).then_inc(s_dve, 1)

            def step(k, par):
                only_cos = isinstance(k, int) and k == 1
                last = isinstance(k, int) and k == 9
                take_mixed(2 * k - 1, 1)
                kernels(2 * k + 1, 1)
                combine(k)
                take_spread(k - 1, 1)
                take_spread(k - 1, 3)
                stationaries((2 * k + 1, 1), 1, k)
                take_mixed(2 * k, 0)
                rests(k, par, 2)
                if not last:
                    kernels(2 * k + 2, 0)
                if not only_cos:
                    take_spread(k - 1, 5)
                if not last:
                    stationaries((2 * k + 2, 0), 0, k + 1)
                third_parts(k, par, 2)
                if not only_cos:
                    take_spread(k - 1, 7)

            dve.wait_ge(modes_in, NB)
            stationaries((0, 0), 0, 0)
            stationaries((1, 1), 1, 10)
            take_mixed(0, 0)
            kernels(2, 0)
            stationaries((2, 0), 0, 1)
            dve.wait_ge(zeroed, 4)
            combine(0)
            rests(0, 0, 1)
            third_parts(0, 0, 1)
            step(1, 1)
            step(2, 0)
            with dve.Fori(0, 3) as i:
                step(2 * i + 3, 1)
                step(2 * i + 4, 0)
            step(9, 1)
            take_mixed(19, 1)
            combine(10)
            take_spread(9, 1)
            rests(10, 0, 2)
            take_spread(9, 3)
            third_parts(10, 0, 2)
            take_spread(9, 5)
            take_spread(9, 7)
            for i in range(1, 8, 2):
                take_spread(10, i)

            def copy_six(b, n, v):
                wait(dve, iw_done, n - 1)
                src = sub(spec[0:SROWS, :], b * SB + 2 * GC * v * ROWS, [[ROWS, 2 * GC], [0, 6], [1, ROWS]])
                exact_copy(copies[:, v % 2, :].rearrange("p (a r k) -> p a r k", r=6, k=ROWS),
                           src).then_inc(copies_in, 1)

            def rest(b, n, v):
                dve.wait_ge(b1_in, n + 1)
                dve.scalar_tensor_tensor(brest[:, v % 2, :], b1[:, v % 2, :], part[:, 0:1],
                                         brest[:, v % 2, :], ALU.mult, ALU.add).then_inc(brest_in, 1)

            def row_part(par, n, v):
                dve.wait_ge(b2_in, n + 1)
                dve.scalar_tensor_tensor(sub(bst[par], GC * v, [[1, GC], [C, W]]),
                                         b2[:, v % 2, :].rearrange("p (c w) -> p c w", c=GC), part[:, 1:2],
                                         brest[:, v % 2, :].rearrange("p (c w) -> p c w", c=GC),
                                         ALU.mult, ALU.add).then_inc(b_in, 1)

            def add_x(b, u):
                j = u // 4
                at = j % SLOTS_3 * TILE + (u % 4) * UNIT
                dve.wait_ge(unit_done, b * UNITS + u + 1)
                dve.tensor_tensor(ring[:, at:at + UNIT], bank[2 + u % 4][:], ring[:, at:at + UNIT],
                                  ALU.add).then_inc(added, 1)

            def inverse(b, par):
                for u in range(UNITS):
                    m = u // 2 + GROUPS
                    if u % 2 == 0:
                        group(lambda _, n, v: row_part(1 - par, n, v), b, m)
                        group(copy_six, b, m + 4)
                    else:
                        group(rest, b, m + 1)
                    add_x(b, u)

            dve.wait_ge(s_act, CHUNKS // 2)
            dve.wait_ge(s_dve, CHUNKS // 2)
            group(copy_six, 0, 0)
            group(copy_six, 0, 1)
            def rest_0(n):
                dve.wait_ge(b1_in, n + 1)
                wait(dve, b_in, n - 1)
                dve.scalar_tensor_tensor(brest[:, n % 2, :], b1[:, n % 2, :], part[:, 0:1],
                                         bank[6 + n % 2][0:BROWS, :], ALU.mult, ALU.add).then_inc(brest_in, 1)

            rest_0(0)
            for n in range(GROUPS):
                group(copy_six, 0, n + 2)
                if n + 1 < GROUPS:
                    rest_0(n + 1)
                row_part(0, n, n)
            group(copy_six, 0, GROUPS + 2)
            group(copy_six, 0, GROUPS + 3)
            group(rest, 0, GROUPS)
            inverse(0, 0)
            with dve.Fori(0, (NB - 4) // 2) as i:
                inverse(2 * i + 1, 1)
                inverse(2 * i + 2, 0)
            for b in range(NB - 3, NB):
                inverse(b, b % 2)


def tables():
    import numpy as np

    def parts(a):
        a = a.astype(np.float32)
        p = []
        for _ in range(3):
            p.append(((a.view(np.uint32) + 0x8000) & 0xFFFF0000).view(np.float32))
            a = a - p[-1]
        return p

    def angle(f, n):
        return 2 * np.pi * (np.outer(f, n) % 256) / 256

    n = np.arange(256)
    k, kx = np.arange(KP), np.arange(KX)
    row_h = np.concatenate([np.cos(angle(k, n)), np.sin(angle(k[1:], n))])
    t_h = np.zeros((P, 2, 32), np.float32)
    t_h[:, :, 0:ROWS] = row_h.reshape(ROWS, 2, P).transpose(2, 1, 0)
    c, s = np.cos(angle(kx, n)), np.sin(angle(kx, n))
    v = np.stack([np.stack([c, c]), np.stack([-s, -s]), np.stack([-s, s]), np.stack([-c, c])])
    t_w = v.reshape(4, 2 * KX, 2, P).transpose(3, 2, 0, 1).astype(np.float32)
    weight = np.where(kx == 0, 1.0, 2.0)[:, None] / (H * W)
    t_iw = np.zeros((SROWS, 2, W), np.float32)
    for odd in range(2):
        order = [4 * kh + 2 * g + odd for h in range(2) for kh in range(h, KH, 2) for g in range(2)]
        g = parts(np.stack([weight * c, -weight * s], 1)[order].reshape(PKX, W))
        t_iw[0:3 * PKX, odd] = np.concatenate([g[0], g[0], g[0]])
        t_iw[SECOND:, odd] = np.concatenate([g[1], g[1], g[2]])
    f = parts(row_h)
    t_ih = np.concatenate([f[0], f[0], f[0], f[1], f[1], f[2]]).reshape(BROWS, 2, P)
    p = np.array([[0, 0], [-1, 0], [-1, -1], [0, 0], [-1, 0], [0, 0]], np.float32)
    t_part = np.repeat(p, ROWS, axis=0)
    t_sel = np.concatenate([np.eye(C), np.eye(C)]).astype(np.float32)
    return dict(t_h=t_h, t_w=t_w, t_id=np.eye(P, dtype=np.float32), t_sel=t_sel, t_iw=t_iw, t_ih=t_ih, t_part=t_part)


def kernel(x, L0_conv_kernel_real, L0_conv_kernel_imag, L0_conv_w_lin):
    import numpy as np
    import concourse.bacc as bacc
    from concourse.bass_utils import run_bass_kernel_spmd

    nc = bacc.Bacc("TRN2", target_bir_lowering=False, num_devices=1)
    given = dict(x=x, k_re=L0_conv_kernel_real, k_im=L0_conv_kernel_imag, w_lin=L0_conv_w_lin)
    arrays, args = {}, {}
    for name, a in {**given, **tables()}.items():
        a = np.ascontiguousarray(a)
        arrays[f"in_{name}"] = a
        args[name] = nc.dram_tensor(f"in_{name}", a.shape, mybir.dt.from_np(a.dtype), kind="ExternalInput").ap()
    args["out"] = nc.dram_tensor("out_y", args["x"].shape, F32, kind="ExternalOutput").ap()
    spectral_conv(nc, **args)
    r = run_bass_kernel_spmd(nc, [arrays], core_ids=[0])
    return r.results[0]["out_y"]
```
